# Optimizing a Trainium2 kernel written in Bass

```python
import numpy as np
import jax
import jax.numpy as jnp

def _softmax(x, axis=-1):
    return jax.nn.softmax(x, axis=axis)

def _gelu(x):
    return jax.nn.gelu(x, approximate=True)

def _silu(x):
    return jax.nn.silu(x)

def _sigmoid(x):
    return jax.nn.sigmoid(x)

def _layernorm(x, axis=-1, eps=1e-05):
    m = jnp.mean(x, axis=axis, keepdims=True)
    v = jnp.var(x, axis=axis, keepdims=True)
    return (x - m) / jnp.sqrt(v + eps)

def _scatter_add(tgt, idx, src, axis=0):
    return tgt.at[idx].add(src)

def _segment_sum(src, seg, n):
    return jax.ops.segment_sum(src, seg, n)
kernel_name = 'mk_adaln_attn_ffn_d2_seqx_r4_b45e8d'

def setup_inputs(seed: int=0):
    np.random.seed(seed)
    _w = jnp.asarray

    def _rec_inputs():
        import jax
        import jax.numpy as jnp
        _rk = jax.random.key(seed)
        x = -0.0002928 + 1 * jax.random.normal(jax.random.fold_in(_rk, 1), (4, 512, 256), jnp.float32)
        _lenS = 512 - jax.random.randint(jax.random.fold_in(_rk, 7), (4,), 0, max(1, 512 // 4) + 1, jnp.int32)
        _lenS2 = 512 - jax.random.randint(jax.random.fold_in(_rk, 8), (4,), 0, max(1, 512 // 4) + 1, jnp.int32)
        cond_64 = -0.0184271 + 1.00439 * jax.random.normal(jax.random.fold_in(_rk, 12), (4, 64), jnp.float32)
        fside_16xSxS_0 = -5.72187e-05 + 0.999849 * jax.random.normal(jax.random.fold_in(_rk, 13), (16, 512, 512), jnp.float32)
        _validS = jnp.arange(512)[None, :] < _lenS[:, None]
        _validS2 = jnp.arange(512)[None, :] < _lenS2[:, None]
        _causal = jnp.tril(jnp.ones((512, 512), dtype=bool))
        mask_BxS_bf1 = jnp.ones((4, 512), dtype=bool)
        mask_BxS_bk0 = jnp.logical_not(jnp.broadcast_to(_validS[:, :], (4, 512)))
        return (x, cond_64, fside_16xSxS_0, mask_BxS_bf1, mask_BxS_bk0)
    x, cond_64, fside_16xSxS_0, mask_BxS_bf1, mask_BxS_bk0 = _rec_inputs()

    def _L0_cond_setup():
        import jax, jax.numpy as jnp
        import numpy as np
        DIM = 256
        HEADS = 16
        DIM_HEAD = 64
        SCALE = 8.0

        def ln(x, g, eps=1e-05):
            mean = x.mean(axis=-1, keepdims=True)
            var = ((x - mean) ** 2).mean(axis=-1, keepdims=True)
            return (x - mean) * jax.lax.rsqrt(var + eps) * g

        def l2norm(t):
            n = jnp.maximum(jnp.linalg.norm(t, axis=-1, keepdims=True), 1e-12)
            return t / n

        def rel_pos_bias(n, w0, b0, g0, w1, b1, g1, w2, b2, dtype):
            pos = jnp.arange(-n + 1, n, dtype=dtype)[:, None]
            h = jax.nn.silu(ln(pos @ w0 + b0, g0))
            h = jax.nn.silu(ln(h @ w1 + b1, g1))
            h = h @ w2 + b2
            i = jnp.arange(n)
            idx = i[:, None] - i[None, :] + n - 1
            bias = h[idx]
            return jnp.transpose(bias, (2, 0, 1))
        key = jax.random.key(seed)
        ks = jax.random.split(key, 16)
        b, n = (2, 512)
        inner = HEADS * DIM_HEAD
        s = 0.02
        return {'x': jax.random.normal(ks[0], (b, n, DIM), jnp.float32), 'mask': jnp.ones((b, n), dtype=bool), 'g_norm': jnp.ones((DIM,), jnp.float32), 'Wq': jax.random.normal(ks[1], (DIM, inner), jnp.float32) * s, 'Wkv': jax.random.normal(ks[2], (DIM, 2 * DIM_HEAD), jnp.float32) * s, 'q_scale': jnp.ones((DIM_HEAD,), jnp.float32), 'k_scale': jnp.ones((DIM_HEAD,), jnp.float32), 'null_kv': jax.random.normal(ks[3], (2, DIM_HEAD), jnp.float32), 'null_attn_bias': jax.random.normal(ks[4], (HEADS,), jnp.float32), 'w0': jax.random.normal(ks[5], (1, DIM), jnp.float32) * s, 'b0': jnp.zeros((DIM,), jnp.float32), 'g0': jnp.ones((DIM,), jnp.float32), 'w1': jax.random.normal(ks[6], (DIM, DIM), jnp.float32) * s, 'b1': jnp.zeros((DIM,), jnp.float32), 'g1': jnp.ones((DIM,), jnp.float32), 'w2': jax.random.normal(ks[7], (DIM, HEADS), jnp.float32) * s, 'b2': jnp.zeros((HEADS,), jnp.float32), 'Wout': jax.random.normal(ks[8], (inner, DIM), jnp.float32) * s, 'g_out': jnp.ones((DIM,), jnp.float32)}
    _L0_cond_all = _L0_cond_setup()
    _L0_cond_in = {k: v for k, v in _L0_cond_all.items() if k in ('g_norm', 'Wq', 'Wkv', 'q_scale', 'k_scale', 'null_attn_bias', 'w0', 'b0', 'g0', 'w1', 'b1', 'g1', 'w2', 'b2', 'Wout', 'g_out')}
    del _L0_cond_all

    def _L0_attn_setup():
        import jax, jax.numpy as jnp
        import numpy as np
        B, S, HID, NH, BS = (1, 512, 256, 16, 64)
        D = HID // NH
        THRESH = 0.01
        SCALE = D ** (-0.5)
        key = jax.random.key(seed)
        ks = jax.random.split(key, 5)
        wscale = 1.0 / np.sqrt(HID)
        x = jax.random.normal(ks[0], (B, S, HID), dtype=jnp.float32)
        wq = jax.random.normal(ks[1], (HID, HID), dtype=jnp.float32) * wscale
        wk = jax.random.normal(ks[2], (HID, HID), dtype=jnp.float32) * wscale
        wv = jax.random.normal(ks[3], (HID, HID), dtype=jnp.float32) * wscale
        wo = jax.random.normal(ks[4], (HID, HID), dtype=jnp.float32) * wscale
        return {'x': x, 'wq': wq, 'wk': wk, 'wv': wv, 'wo': wo}
    _L0_attn_all = _L0_attn_setup()
    _L0_attn_in = {k: v for k, v in _L0_attn_all.items() if k in ('wq', 'wk', 'wv', 'wo')}
    del _L0_attn_all

    def _L0_cond2_setup():
        import jax, jax.numpy as jnp
        import numpy as np
        B, S, H = (4, 512, 256)
        E = 8
        M = 128
        K = 2
        N_SHARED = 2
        SM = M * N_SHARED
        G = 64
        GE_TEMP = 1.0
        ALPHA = 0.001
        SEQ_AUX = True
        NORM_TOPK = True
        COS_TEMP = 0.78
        CONS_ALPHA = 0.01
        LEAKY_SLOPE = 0.01
        EPS_COS = 1e-08

        def _leaky(x):
            return jnp.where(x >= 0, x, LEAKY_SLOPE * x)

        def _moe_forward(hidden_states, g, wt, wg, w_gate, w_up, w_down, sw_gate, sw_up, sw_down):
            b, s, h = hidden_states.shape
            x = hidden_states.reshape(-1, h)
            T = x.shape[0]
            logits_h = x @ wt.T
            logits_g = g @ wg.T
            logits_g = jnp.repeat(logits_g, s, axis=0)
            logits = (logits_h + logits_g / GE_TEMP) / (1.0 + 1.0 / GE_TEMP)
            scores = jax.nn.softmax(logits, axis=-1)
            topk_w, topk_idx = jax.lax.top_k(scores, K)
            if K > 1 and NORM_TOPK:
                topk_w = topk_w / (topk_w.sum(-1, keepdims=True) + 1e-20)
            onehot = jax.nn.one_hot(topk_idx.reshape(b, s * K), E, dtype=jnp.float32)
            ce = onehot.sum(1) / (s * K / E)
            aux_loss = (ce * scores.reshape(b, s, E).mean(1)).sum(1).mean() * ALPHA
            gp = _leaky(jnp.einsum('th,ehm->etm', x, w_gate))
            up = jnp.einsum('th,ehm->etm', x, w_up)
            y_all = jnp.einsum('etm,emh->eth', gp * up, w_down)
            y_sel = y_all[topk_idx, jnp.arange(T)[:, None], :]
            y = (y_sel * topk_w[..., None]).sum(1).reshape(b, s, h)
            p = _leaky(hidden_states @ sw_gate) * (hidden_states @ sw_up) @ sw_down
            y = y + p
            num = jnp.sum(y * p, -1)
            den = jnp.maximum(jnp.linalg.norm(y, axis=-1), EPS_COS) * jnp.maximum(jnp.linalg.norm(p, axis=-1), EPS_COS)
            closs = CONS_ALPHA * jnp.mean(num / den / (1.0 + COS_TEMP))
            return (y, aux_loss + closs)
        key = jax.random.key(seed)
        ks = jax.random.split(key, 12)
        sh = 1.0 / np.sqrt(H)
        sm = 1.0 / np.sqrt(M)
        ssm = 1.0 / np.sqrt(SM)
        sg = 1.0 / np.sqrt(G)
        return {'hidden_states': jax.random.normal(ks[0], (B, S, H), jnp.float32), 'g': jax.random.normal(ks[1], (B, G), jnp.float32), 'wt': jax.random.uniform(ks[2], (E, H), jnp.float32, -sh, sh), 'wg': jax.random.uniform(ks[3], (E, G), jnp.float32, -sg, sg), 'w_gate': jax.random.uniform(ks[4], (E, H, M), jnp.float32, -sh, sh), 'w_up': jax.random.uniform(ks[5], (E, H, M), jnp.float32, -sh, sh), 'w_down': jax.random.uniform(ks[6], (E, M, H), jnp.float32, -sm, sm), 'sw_gate': jax.random.uniform(ks[7], (H, SM), jnp.float32, -sh, sh), 'sw_up': jax.random.uniform(ks[8], (H, SM), jnp.float32, -sh, sh), 'sw_down': jax.random.uniform(ks[9], (SM, H), jnp.float32, -ssm, ssm)}
    _L0_cond2_all = _L0_cond2_setup()
    _L0_cond2_in = {k: v for k, v in _L0_cond2_all.items() if k in ('wt', 'wg', 'w_gate', 'w_up', 'w_down', 'sw_gate', 'sw_up', 'sw_down')}
    del _L0_cond2_all

    def _L0_ffn_setup():
        import jax, jax.numpy as jnp
        import numpy as np
        D_IN, D_HID = (256, 1024)

        def _ternary(key, shape):
            return jax.random.randint(key, shape, -1, 2).astype(jnp.float32)

        def _tlin(x, w, s):
            return jnp.einsum('bsi,oi->bso', x, w) * s
        key = jax.random.key(seed)
        ks = jax.random.split(key, 12)
        inv = lambda fan: 1.0 / np.sqrt(fan).astype(np.float32)
        return {'x': jax.random.normal(ks[0], (4, 512, D_IN), dtype=jnp.float32), 'w1_w': _ternary(ks[1], (D_HID, D_IN)), 'w1_s': jax.random.uniform(ks[2], (D_HID,), dtype=jnp.float32) * inv(D_IN), 'w2_w': _ternary(ks[3], (D_HID, D_IN)), 'w2_s': jax.random.uniform(ks[4], (D_HID,), dtype=jnp.float32) * inv(D_IN), 'h1_w': _ternary(ks[5], (D_HID, D_HID)), 'h1_s': jax.random.uniform(ks[6], (D_HID,), dtype=jnp.float32) * inv(D_HID), 'h2_w': _ternary(ks[7], (D_HID, D_HID)), 'h2_s': jax.random.uniform(ks[8], (D_HID,), dtype=jnp.float32) * inv(D_HID), 'w3_w': _ternary(ks[9], (D_IN, D_HID)), 'w3_s': jax.random.uniform(ks[10], (D_IN,), dtype=jnp.float32) * inv(D_HID)}
    _L0_ffn_all = _L0_ffn_setup()
    _L0_ffn_in = {k: v for k, v in _L0_ffn_all.items() if k in ('w1_w', 'w1_s', 'w2_w', 'w2_s', 'h1_w', 'h1_s', 'h2_w', 'h2_s', 'w3_w', 'w3_s')}
    del _L0_ffn_all

    def _L1_cond_setup():
        import jax, jax.numpy as jnp
        import numpy as np
        B, N, DIM, H, DH = (2, 512, 256, 16, 64)
        INNER = H * DH
        EPS = 1e-05

        def layernorm(x, g):
            mean = jnp.mean(x, axis=-1, keepdims=True)
            var = jnp.var(x, axis=-1, keepdims=True)
            return (x - mean) * jax.lax.rsqrt(var + EPS) * g
        key = jax.random.key(seed)
        ks = jax.random.split(key, 10)
        x = jax.random.normal(ks[0], (B, N, DIM), dtype=jnp.float32)
        attn_bias = jax.random.normal(ks[1], (H, N, N), dtype=jnp.float32)
        mask = jax.random.randint(ks[2], (B, N), 0, 2).astype(bool)
        g_in = jnp.ones((DIM,), dtype=jnp.float32)
        null_attn_bias = jax.random.normal(ks[3], (H,), dtype=jnp.float32)
        null_kv = jax.random.normal(ks[4], (2, DH), dtype=jnp.float32)
        Wq = jax.random.normal(ks[5], (DIM, INNER), dtype=jnp.float32) * 0.02
        Wkv = jax.random.normal(ks[6], (DIM, 2 * DH), dtype=jnp.float32) * 0.02
        Wo = jax.random.normal(ks[7], (INNER, DIM), dtype=jnp.float32) * 0.02
        g_out = jnp.ones((DIM,), dtype=jnp.float32)
        return {'x': x, 'attn_bias': attn_bias, 'mask': mask, 'g_in': g_in, 'null_attn_bias': null_attn_bias, 'null_kv': null_kv, 'Wq': Wq, 'Wkv': Wkv, 'Wo': Wo, 'g_out': g_out}
    _L1_cond_all = _L1_cond_setup()
    _L1_cond_in = {k: v for k, v in _L1_cond_all.items() if k in ('g_in', 'null_attn_bias', 'Wq', 'Wkv', 'Wo', 'g_out')}
    del _L1_cond_all

    def _L1_attn_setup():
        import jax, jax.numpy as jnp
        import numpy as np
        EMBED_DIM = 256
        NUM_HEADS = 16
        CHUNK_SIZE = 128
        BATCH = 4
        SEQ_LEN = 2048

        def _chunked_attention(x, wq, bq, wk, bk, wv, bv, wo, bo):
            B, S, E = x.shape
            H, T = (NUM_HEADS, CHUNK_SIZE)
            D = E // H
            C = S // T
            scale = 1.0 / float(np.sqrt(D))

            def proj(w, b):
                y = jnp.einsum('bse,fe->bsf', x, w) + b
                return y.reshape(B, C, T, H, D).transpose(0, 3, 1, 2, 4)
            q = proj(wq, bq)
            k = proj(wk, bk)
            v = proj(wv, bv)
            s_intra = jnp.einsum('bhctd,bhcsd->bhcts', q, k) * scale
            a_intra = jax.nn.softmax(s_intra, axis=-1)
            intra = jnp.einsum('bhcts,bhcsd->bhctd', a_intra, v)
            k_means = k.mean(axis=3)
            v_means = v.mean(axis=3)
            s_inter = jnp.einsum('bhctd,bhjd->bhctj', q, k_means) * scale
            chunk_pos = jnp.arange(C)
            causal = chunk_pos[:, None] >= chunk_pos[None, :]
            s_inter = jnp.where(causal[None, None, :, None, :], s_inter, -jnp.inf)
            a_inter = jax.nn.softmax(s_inter, axis=-1)
            inter = jnp.einsum('bhctj,bhjd->bhctd', a_inter, v_means)
            out = intra + inter
            out = out.transpose(0, 2, 3, 1, 4).reshape(B, S, E)
            return jnp.einsum('bse,fe->bsf', out, wo) + bo
        key = jax.random.key(seed)
        ks = jax.random.split(key, 9)
        E = EMBED_DIM
        s = 1.0 / np.sqrt(E)
        inp = {'hidden_states': jax.random.normal(ks[0], (BATCH, SEQ_LEN, E), dtype=jnp.float32), 'wq': jax.random.normal(ks[1], (E, E), dtype=jnp.float32) * s, 'bq': jax.random.normal(ks[2], (E,), dtype=jnp.float32) * s, 'wk': jax.random.normal(ks[3], (E, E), dtype=jnp.float32) * s, 'bk': jax.random.normal(ks[4], (E,), dtype=jnp.float32) * s, 'wv': jax.random.normal(ks[5], (E, E), dtype=jnp.float32) * s, 'bv': jax.random.normal(ks[6], (E,), dtype=jnp.float32) * s, 'wo': jax.random.normal(ks[7], (E, E), dtype=jnp.float32) * s, 'bo': jax.random.normal(ks[8], (E,), dtype=jnp.float32) * s}
        return inp
    _L1_attn_all = _L1_attn_setup()
    _L1_attn_in = {k: v for k, v in _L1_attn_all.items() if k in ('wq', 'bq', 'wk', 'bk', 'wv', 'bv', 'wo', 'bo')}
    del _L1_attn_all

    def _L1_cond2_setup():
        import jax, jax.numpy as jnp
        import numpy as np
        B, S, H = (4, 512, 256)
        E = 8
        M = 128
        K = 2
        N_SHARED = 2
        SM = M * N_SHARED
        G = 64
        GE_TEMP = 1.0
        ALPHA = 0.001
        SEQ_AUX = True
        NORM_TOPK = True
        COS_TEMP = 0.78
        CONS_ALPHA = 0.01
        LEAKY_SLOPE = 0.01
        EPS_COS = 1e-08

        def _leaky(x):
            return jnp.where(x >= 0, x, LEAKY_SLOPE * x)

        def _moe_forward(hidden_states, g, wt, wg, w_gate, w_up, w_down, sw_gate, sw_up, sw_down):
            b, s, h = hidden_states.shape
            x = hidden_states.reshape(-1, h)
            T = x.shape[0]
            logits_h = x @ wt.T
            logits_g = g @ wg.T
            logits_g = jnp.repeat(logits_g, s, axis=0)
            logits = (logits_h + logits_g / GE_TEMP) / (1.0 + 1.0 / GE_TEMP)
            scores = jax.nn.softmax(logits, axis=-1)
            topk_w, topk_idx = jax.lax.top_k(scores, K)
            if K > 1 and NORM_TOPK:
                topk_w = topk_w / (topk_w.sum(-1, keepdims=True) + 1e-20)
            onehot = jax.nn.one_hot(topk_idx.reshape(b, s * K), E, dtype=jnp.float32)
            ce = onehot.sum(1) / (s * K / E)
            aux_loss = (ce * scores.reshape(b, s, E).mean(1)).sum(1).mean() * ALPHA
            gp = _leaky(jnp.einsum('th,ehm->etm', x, w_gate))
            up = jnp.einsum('th,ehm->etm', x, w_up)
            y_all = jnp.einsum('etm,emh->eth', gp * up, w_down)
            y_sel = y_all[topk_idx, jnp.arange(T)[:, None], :]
            y = (y_sel * topk_w[..., None]).sum(1).reshape(b, s, h)
            p = _leaky(hidden_states @ sw_gate) * (hidden_states @ sw_up) @ sw_down
            y = y + p
            num = jnp.sum(y * p, -1)
            den = jnp.maximum(jnp.linalg.norm(y, axis=-1), EPS_COS) * jnp.maximum(jnp.linalg.norm(p, axis=-1), EPS_COS)
            closs = CONS_ALPHA * jnp.mean(num / den / (1.0 + COS_TEMP))
            return (y, aux_loss + closs)
        key = jax.random.key(seed)
        ks = jax.random.split(key, 12)
        sh = 1.0 / np.sqrt(H)
        sm = 1.0 / np.sqrt(M)
        ssm = 1.0 / np.sqrt(SM)
        sg = 1.0 / np.sqrt(G)
        return {'hidden_states': jax.random.normal(ks[0], (B, S, H), jnp.float32), 'g': jax.random.normal(ks[1], (B, G), jnp.float32), 'wt': jax.random.uniform(ks[2], (E, H), jnp.float32, -sh, sh), 'wg': jax.random.uniform(ks[3], (E, G), jnp.float32, -sg, sg), 'w_gate': jax.random.uniform(ks[4], (E, H, M), jnp.float32, -sh, sh), 'w_up': jax.random.uniform(ks[5], (E, H, M), jnp.float32, -sh, sh), 'w_down': jax.random.uniform(ks[6], (E, M, H), jnp.float32, -sm, sm), 'sw_gate': jax.random.uniform(ks[7], (H, SM), jnp.float32, -sh, sh), 'sw_up': jax.random.uniform(ks[8], (H, SM), jnp.float32, -sh, sh), 'sw_down': jax.random.uniform(ks[9], (SM, H), jnp.float32, -ssm, ssm)}
    _L1_cond2_all = _L1_cond2_setup()
    _L1_cond2_in = {k: v for k, v in _L1_cond2_all.items() if k in ('wt', 'wg', 'w_gate', 'w_up', 'w_down', 'sw_gate', 'sw_up', 'sw_down')}
    del _L1_cond2_all

    def _L1_ffn_setup():
        import jax, jax.numpy as jnp
        import numpy as np
        B, S, D, H, F = (4, 1024, 256, 16, 1024)
        CAP = 0.125
        ROPE_BASE = 10000.0

        def rmsnorm(x, g):
            return x * jax.lax.rsqrt(jnp.mean(x * x, -1, keepdims=True) + 1e-06) * g

        def rope(t, pos):
            hd = t.shape[-1]
            inv = 1.0 / ROPE_BASE ** (jnp.arange(0, hd, 2, dtype=jnp.float32) / hd)
            f = pos[:, None, :, None].astype(jnp.float32) * inv
            emb = jnp.concatenate([f, f], axis=-1)
            cos, sin = (jnp.cos(emb), jnp.sin(emb))
            rot = jnp.concatenate([-t[..., hd // 2:], t[..., :hd // 2]], axis=-1)
            return t * cos + rot * sin
        key = jax.random.key(seed)
        ks = jax.random.split(key, 9)
        scale = 0.02
        x = jax.random.normal(ks[0], (B, S, D), jnp.float32)
        causal = jnp.where(jnp.tril(jnp.ones((S, S), bool)), 0.0, -1000000000.0).astype(jnp.float32)
        attention_mask = jnp.broadcast_to(causal[None, None], (B, 1, S, S))
        position_ids = jnp.broadcast_to(jnp.arange(S, dtype=jnp.int32), (B, S))
        return {'x': x, 'attention_mask': attention_mask, 'position_ids': position_ids, 'router_w': jax.random.normal(ks[1], (D, 1), jnp.float32) * scale, 'router_b': jnp.zeros((1,), jnp.float32), 'wq': jax.random.normal(ks[2], (D, D), jnp.float32) * scale, 'wk': jax.random.normal(ks[3], (D, D), jnp.float32) * scale, 'wv': jax.random.normal(ks[4], (D, D), jnp.float32) * scale, 'wo': jax.random.normal(ks[5], (D, D), jnp.float32) * scale, 'w1': jax.random.normal(ks[6], (D, F), jnp.float32) * scale, 'w2': jax.random.normal(ks[7], (F, D), jnp.float32) * scale, 'ln1': jnp.ones((D,), jnp.float32), 'ln2': jnp.ones((D,), jnp.float32)}
    _L1_ffn_all = _L1_ffn_setup()
    _L1_ffn_in = {k: v for k, v in _L1_ffn_all.items() if k in ('attention_mask', 'position_ids', 'router_w', 'router_b', 'wq', 'wk', 'wv', 'wo', 'w1', 'w2', 'ln1', 'ln2')}
    del _L1_ffn_all
    return {'x': x, 'cond_64': cond_64, 'fside_16xSxS_0': fside_16xSxS_0, 'mask_BxS_bf1': mask_BxS_bf1, 'mask_BxS_bk0': mask_BxS_bk0, 'L0_cond_g_norm': _L0_cond_in['g_norm'], 'L0_cond_Wq': _L0_cond_in['Wq'], 'L0_cond_Wkv': _L0_cond_in['Wkv'], 'L0_cond_q_scale': _L0_cond_in['q_scale'], 'L0_cond_k_scale': _L0_cond_in['k_scale'], 'L0_cond_null_attn_bias': _L0_cond_in['null_attn_bias'], 'L0_cond_w0': _L0_cond_in['w0'], 'L0_cond_b0': _L0_cond_in['b0'], 'L0_cond_g0': _L0_cond_in['g0'], 'L0_cond_w1': _L0_cond_in['w1'], 'L0_cond_b1': _L0_cond_in['b1'], 'L0_cond_g1': _L0_cond_in['g1'], 'L0_cond_w2': _L0_cond_in['w2'], 'L0_cond_b2': _L0_cond_in['b2'], 'L0_cond_Wout': _L0_cond_in['Wout'], 'L0_cond_g_out': _L0_cond_in['g_out'], 'L0_attn_wq': _L0_attn_in['wq'], 'L0_attn_wk': _L0_attn_in['wk'], 'L0_attn_wv': _L0_attn_in['wv'], 'L0_attn_wo': _L0_attn_in['wo'], 'L0_cond2_wt': _L0_cond2_in['wt'], 'L0_cond2_wg': _L0_cond2_in['wg'], 'L0_cond2_w_gate': _L0_cond2_in['w_gate'], 'L0_cond2_w_up': _L0_cond2_in['w_up'], 'L0_cond2_w_down': _L0_cond2_in['w_down'], 'L0_cond2_sw_gate': _L0_cond2_in['sw_gate'], 'L0_cond2_sw_up': _L0_cond2_in['sw_up'], 'L0_cond2_sw_down': _L0_cond2_in['sw_down'], 'L0_ffn_w1_w': _L0_ffn_in['w1_w'], 'L0_ffn_w1_s': _L0_ffn_in['w1_s'], 'L0_ffn_w2_w': _L0_ffn_in['w2_w'], 'L0_ffn_w2_s': _L0_ffn_in['w2_s'], 'L0_ffn_h1_w': _L0_ffn_in['h1_w'], 'L0_ffn_h1_s': _L0_ffn_in['h1_s'], 'L0_ffn_h2_w': _L0_ffn_in['h2_w'], 'L0_ffn_h2_s': _L0_ffn_in['h2_s'], 'L0_ffn_w3_w': _L0_ffn_in['w3_w'], 'L0_ffn_w3_s': _L0_ffn_in['w3_s'], 'L1_cond_g_in': _L1_cond_in['g_in'], 'L1_cond_null_attn_bias': _L1_cond_in['null_attn_bias'], 'L1_cond_Wq': _L1_cond_in['Wq'], 'L1_cond_Wkv': _L1_cond_in['Wkv'], 'L1_cond_Wo': _L1_cond_in['Wo'], 'L1_cond_g_out': _L1_cond_in['g_out'], 'L1_attn_wq': _L1_attn_in['wq'], 'L1_attn_bq': _L1_attn_in['bq'], 'L1_attn_wk': _L1_attn_in['wk'], 'L1_attn_bk': _L1_attn_in['bk'], 'L1_attn_wv': _L1_attn_in['wv'], 'L1_attn_bv': _L1_attn_in['bv'], 'L1_attn_wo': _L1_attn_in['wo'], 'L1_attn_bo': _L1_attn_in['bo'], 'L1_cond2_wt': _L1_cond2_in['wt'], 'L1_cond2_wg': _L1_cond2_in['wg'], 'L1_cond2_w_gate': _L1_cond2_in['w_gate'], 'L1_cond2_w_up': _L1_cond2_in['w_up'], 'L1_cond2_w_down': _L1_cond2_in['w_down'], 'L1_cond2_sw_gate': _L1_cond2_in['sw_gate'], 'L1_cond2_sw_up': _L1_cond2_in['sw_up'], 'L1_cond2_sw_down': _L1_cond2_in['sw_down'], 'L1_ffn_attention_mask': _L1_ffn_in['attention_mask'], 'L1_ffn_position_ids': _L1_ffn_in['position_ids'], 'L1_ffn_router_w': _L1_ffn_in['router_w'], 'L1_ffn_router_b': _L1_ffn_in['router_b'], 'L1_ffn_wq': _L1_ffn_in['wq'], 'L1_ffn_wk': _L1_ffn_in['wk'], 'L1_ffn_wv': _L1_ffn_in['wv'], 'L1_ffn_wo': _L1_ffn_in['wo'], 'L1_ffn_w1': _L1_ffn_in['w1'], 'L1_ffn_w2': _L1_ffn_in['w2'], 'L1_ffn_ln1': _L1_ffn_in['ln1'], 'L1_ffn_ln2': _L1_ffn_in['ln2']}

def reference(x, cond_64, fside_16xSxS_0, mask_BxS_bf1, mask_BxS_bk0, L0_cond_g_norm, L0_cond_Wq, L0_cond_Wkv, L0_cond_q_scale, L0_cond_k_scale, L0_cond_null_attn_bias, L0_cond_w0, L0_cond_b0, L0_cond_g0, L0_cond_w1, L0_cond_b1, L0_cond_g1, L0_cond_w2, L0_cond_b2, L0_cond_Wout, L0_cond_g_out, L0_attn_wq, L0_attn_wk, L0_attn_wv, L0_attn_wo, L0_cond2_wt, L0_cond2_wg, L0_cond2_w_gate, L0_cond2_w_up, L0_cond2_w_down, L0_cond2_sw_gate, L0_cond2_sw_up, L0_cond2_sw_down, L0_ffn_w1_w, L0_ffn_w1_s, L0_ffn_w2_w, L0_ffn_w2_s, L0_ffn_h1_w, L0_ffn_h1_s, L0_ffn_h2_w, L0_ffn_h2_s, L0_ffn_w3_w, L0_ffn_w3_s, L1_cond_g_in, L1_cond_null_attn_bias, L1_cond_Wq, L1_cond_Wkv, L1_cond_Wo, L1_cond_g_out, L1_attn_wq, L1_attn_bq, L1_attn_wk, L1_attn_bk, L1_attn_wv, L1_attn_bv, L1_attn_wo, L1_attn_bo, L1_cond2_wt, L1_cond2_wg, L1_cond2_w_gate, L1_cond2_w_up, L1_cond2_w_down, L1_cond2_sw_gate, L1_cond2_sw_up, L1_cond2_sw_down, L1_ffn_attention_mask, L1_ffn_position_ids, L1_ffn_router_w, L1_ffn_router_b, L1_ffn_wq, L1_ffn_wk, L1_ffn_wv, L1_ffn_wo, L1_ffn_w1, L1_ffn_w2, L1_ffn_ln1, L1_ffn_ln2):
    import jax
    import jax.numpy as jnp

    def _L0_cond_ref(x, mask, g_norm, Wq, Wkv, q_scale, k_scale, null_kv, null_attn_bias, w0, b0, g0, w1, b1, g1, w2, b2, Wout, g_out):
        import jax, jax.numpy as jnp
        import numpy as np
        DIM = 256
        HEADS = 16
        DIM_HEAD = 64
        SCALE = 8.0

        def ln(x, g, eps=1e-05):
            mean = x.mean(axis=-1, keepdims=True)
            var = ((x - mean) ** 2).mean(axis=-1, keepdims=True)
            return (x - mean) * jax.lax.rsqrt(var + eps) * g

        def l2norm(t):
            n = jnp.maximum(jnp.linalg.norm(t, axis=-1, keepdims=True), 1e-12)
            return t / n

        def rel_pos_bias(n, w0, b0, g0, w1, b1, g1, w2, b2, dtype):
            pos = jnp.arange(-n + 1, n, dtype=dtype)[:, None]
            h = jax.nn.silu(ln(pos @ w0 + b0, g0))
            h = jax.nn.silu(ln(h @ w1 + b1, g1))
            h = h @ w2 + b2
            i = jnp.arange(n)
            idx = i[:, None] - i[None, :] + n - 1
            bias = h[idx]
            return jnp.transpose(bias, (2, 0, 1))
        b, n, _ = x.shape
        xn = ln(x, g_norm)
        q = (xn @ Wq).reshape(b, n, HEADS, DIM_HEAD).transpose(0, 2, 1, 3)
        kv = xn @ Wkv
        k, v = (kv[..., :DIM_HEAD], kv[..., DIM_HEAD:])
        nk = jnp.broadcast_to(null_kv[0], (b, 1, DIM_HEAD))
        nv = jnp.broadcast_to(null_kv[1], (b, 1, DIM_HEAD))
        k = jnp.concatenate([nk, k], axis=1)
        v = jnp.concatenate([nv, v], axis=1)
        q = l2norm(q) * q_scale
        k = l2norm(k) * k_scale
        sim = jnp.einsum('bhid,bjd->bhij', q, k) * SCALE
        bias = rel_pos_bias(n, w0, b0, g0, w1, b1, g1, w2, b2, q.dtype)
        null_bias = jnp.broadcast_to(null_attn_bias[:, None, None], (HEADS, n, 1))
        attn_bias = jnp.concatenate([null_bias, bias], axis=-1)
        sim = sim + attn_bias
        neg = -jnp.finfo(sim.dtype).max
        causal = jnp.triu(jnp.ones((n, n + 1), dtype=bool), k=2)
        sim = jnp.where(causal, neg, sim)
        m = jnp.pad(mask, ((0, 0), (1, 0)), constant_values=True)[:, None, None, :]
        sim = jnp.where(m, sim, neg)
        attn = jax.nn.softmax(sim, axis=-1)
        out = jnp.einsum('bhij,bjd->bhid', attn, v)
        out = out.transpose(0, 2, 1, 3).reshape(b, n, HEADS * DIM_HEAD)
        return ln(out @ Wout, g_out)

    def _L0_attn_ref(x, wq, wk, wv, wo):
        import jax, jax.numpy as jnp
        import numpy as np
        B, S, HID, NH, BS = (1, 512, 256, 16, 64)
        D = HID // NH
        THRESH = 0.01
        SCALE = D ** (-0.5)
        b, s, _ = x.shape
        nb = s // BS

        def proj(w):
            return (x @ w.T).reshape(b, s, NH, D).transpose(0, 2, 1, 3)
        q, k, v = (proj(wq), proj(wk), proj(wv))
        q_mean = q.reshape(b, NH, nb, BS, D).mean(axis=3)
        k_mean = k.reshape(b, NH, nb, BS, D).mean(axis=3)
        block_scores = jnp.einsum('bhid,bhjd->bhij', q_mean, k_mean) / np.sqrt(D)
        block_mask = block_scores > THRESH
        full_mask = jnp.broadcast_to(block_mask[:, :, :, None, :, None], (b, NH, nb, BS, nb, BS)).reshape(b, NH, s, s)
        eye = jnp.eye(s, dtype=bool)
        full_mask = full_mask | eye
        scores = jnp.einsum('bhid,bhjd->bhij', q, k) * SCALE
        scores = jnp.where(full_mask, scores, -jnp.inf)
        attn = jax.nn.softmax(scores, axis=-1)
        block_max = attn.reshape(b, NH, nb, BS, nb, BS).max(axis=(3, 5))
        smask = block_max > THRESH
        sfull = jnp.broadcast_to(smask[:, :, :, None, :, None], (b, NH, nb, BS, nb, BS)).reshape(b, NH, s, s) | eye
        attn = jnp.where(sfull, attn, 0.0)
        out = jnp.einsum('bhij,bhjd->bhid', attn, v)
        out = out.transpose(0, 2, 1, 3).reshape(b, s, NH * D)
        return out @ wo.T

    def _L0_cond2_ref(hidden_states, g, wt, wg, w_gate, w_up, w_down, sw_gate, sw_up, sw_down):
        import jax, jax.numpy as jnp
        import numpy as np
        B, S, H = (4, 512, 256)
        E = 8
        M = 128
        K = 2
        N_SHARED = 2
        SM = M * N_SHARED
        G = 64
        GE_TEMP = 1.0
        ALPHA = 0.001
        SEQ_AUX = True
        NORM_TOPK = True
        COS_TEMP = 0.78
        CONS_ALPHA = 0.01
        LEAKY_SLOPE = 0.01
        EPS_COS = 1e-08

        def _leaky(x):
            return jnp.where(x >= 0, x, LEAKY_SLOPE * x)

        def _moe_forward(hidden_states, g, wt, wg, w_gate, w_up, w_down, sw_gate, sw_up, sw_down):
            b, s, h = hidden_states.shape
            x = hidden_states.reshape(-1, h)
            T = x.shape[0]
            logits_h = x @ wt.T
            logits_g = g @ wg.T
            logits_g = jnp.repeat(logits_g, s, axis=0)
            logits = (logits_h + logits_g / GE_TEMP) / (1.0 + 1.0 / GE_TEMP)
            scores = jax.nn.softmax(logits, axis=-1)
            topk_w, topk_idx = jax.lax.top_k(scores, K)
            if K > 1 and NORM_TOPK:
                topk_w = topk_w / (topk_w.sum(-1, keepdims=True) + 1e-20)
            onehot = jax.nn.one_hot(topk_idx.reshape(b, s * K), E, dtype=jnp.float32)
            ce = onehot.sum(1) / (s * K / E)
            aux_loss = (ce * scores.reshape(b, s, E).mean(1)).sum(1).mean() * ALPHA
            gp = _leaky(jnp.einsum('th,ehm->etm', x, w_gate))
            up = jnp.einsum('th,ehm->etm', x, w_up)
            y_all = jnp.einsum('etm,emh->eth', gp * up, w_down)
            y_sel = y_all[topk_idx, jnp.arange(T)[:, None], :]
            y = (y_sel * topk_w[..., None]).sum(1).reshape(b, s, h)
            p = _leaky(hidden_states @ sw_gate) * (hidden_states @ sw_up) @ sw_down
            y = y + p
            num = jnp.sum(y * p, -1)
            den = jnp.maximum(jnp.linalg.norm(y, axis=-1), EPS_COS) * jnp.maximum(jnp.linalg.norm(p, axis=-1), EPS_COS)
            closs = CONS_ALPHA * jnp.mean(num / den / (1.0 + COS_TEMP))
            return (y, aux_loss + closs)
        y, _ = _moe_forward(hidden_states, g, wt, wg, w_gate, w_up, w_down, sw_gate, sw_up, sw_down)
        return y

    def _L0_ffn_ref(x, w1_w, w1_s, w2_w, w2_s, h1_w, h1_s, h2_w, h2_s, w3_w, w3_s):
        import jax, jax.numpy as jnp
        import numpy as np
        D_IN, D_HID = (256, 1024)

        def _ternary(key, shape):
            return jax.random.randint(key, shape, -1, 2).astype(jnp.float32)

        def _tlin(x, w, s):
            return jnp.einsum('bsi,oi->bso', x, w) * s
        h = jax.nn.silu(_tlin(x, w1_w, w1_s)) * _tlin(x, w2_w, w2_s)
        h = jax.nn.gelu(_tlin(h, h1_w, h1_s), approximate=False)
        h = jax.nn.gelu(_tlin(h, h2_w, h2_s), approximate=False)
        return _tlin(h, w3_w, w3_s)

    def _L1_cond_ref(x, attn_bias, mask, g_in, null_attn_bias, null_kv, Wq, Wkv, Wo, g_out):
        import jax, jax.numpy as jnp
        import numpy as np
        B, N, DIM, H, DH = (2, 512, 256, 16, 64)
        INNER = H * DH
        EPS = 1e-05

        def layernorm(x, g):
            mean = jnp.mean(x, axis=-1, keepdims=True)
            var = jnp.var(x, axis=-1, keepdims=True)
            return (x - mean) * jax.lax.rsqrt(var + EPS) * g
        b, n, _ = x.shape
        scale = DH ** (-0.5)
        xn = layernorm(x, g_in)
        q = (xn @ Wq).reshape(b, n, H, DH).transpose(0, 2, 1, 3) * scale
        kv = xn @ Wkv
        k, v = (kv[..., :DH], kv[..., DH:])
        nk = jnp.broadcast_to(null_kv[0], (b, 1, DH))
        nv = jnp.broadcast_to(null_kv[1], (b, 1, DH))
        k = jnp.concatenate([nk, k], axis=1)
        v = jnp.concatenate([nv, v], axis=1)
        sim = jnp.einsum('bhid,bjd->bhij', q, k)
        null_col = jnp.broadcast_to(null_attn_bias[:, None, None], (H, n, 1))
        bias = jnp.concatenate([null_col, attn_bias], axis=-1)
        sim = sim + bias
        neg = -jnp.finfo(sim.dtype).max
        j = n + 1
        causal_mask = jnp.triu(jnp.ones((n, j), dtype=bool), k=j - n + 1)
        sim = jnp.where(causal_mask, neg, sim)
        mask_p = jnp.pad(mask, ((0, 0), (1, 0)), constant_values=True)
        sim = jnp.where(mask_p[:, None, None, :], sim, neg)
        attn = jax.nn.softmax(sim, axis=-1)
        out = jnp.einsum('bhij,bjd->bhid', attn, v)
        out = out.transpose(0, 2, 1, 3).reshape(b, n, INNER)
        out = out @ Wo
        return layernorm(out, g_out)

    def _L1_attn_ref(hidden_states, wq, bq, wk, bk, wv, bv, wo, bo):
        import jax, jax.numpy as jnp
        import numpy as np
        EMBED_DIM = 256
        NUM_HEADS = 16
        CHUNK_SIZE = 128
        BATCH = 4
        SEQ_LEN = 2048

        def _chunked_attention(x, wq, bq, wk, bk, wv, bv, wo, bo):
            B, S, E = x.shape
            H, T = (NUM_HEADS, CHUNK_SIZE)
            D = E // H
            C = S // T
            scale = 1.0 / float(np.sqrt(D))

            def proj(w, b):
                y = jnp.einsum('bse,fe->bsf', x, w) + b
                return y.reshape(B, C, T, H, D).transpose(0, 3, 1, 2, 4)
            q = proj(wq, bq)
            k = proj(wk, bk)
            v = proj(wv, bv)
            s_intra = jnp.einsum('bhctd,bhcsd->bhcts', q, k) * scale
            a_intra = jax.nn.softmax(s_intra, axis=-1)
            intra = jnp.einsum('bhcts,bhcsd->bhctd', a_intra, v)
            k_means = k.mean(axis=3)
            v_means = v.mean(axis=3)
            s_inter = jnp.einsum('bhctd,bhjd->bhctj', q, k_means) * scale
            chunk_pos = jnp.arange(C)
            causal = chunk_pos[:, None] >= chunk_pos[None, :]
            s_inter = jnp.where(causal[None, None, :, None, :], s_inter, -jnp.inf)
            a_inter = jax.nn.softmax(s_inter, axis=-1)
            inter = jnp.einsum('bhctj,bhjd->bhctd', a_inter, v_means)
            out = intra + inter
            out = out.transpose(0, 2, 3, 1, 4).reshape(B, S, E)
            return jnp.einsum('bse,fe->bsf', out, wo) + bo
        return _chunked_attention(hidden_states, wq, bq, wk, bk, wv, bv, wo, bo)

    def _L1_cond2_ref(hidden_states, g, wt, wg, w_gate, w_up, w_down, sw_gate, sw_up, sw_down):
        import jax, jax.numpy as jnp
        import numpy as np
        B, S, H = (4, 512, 256)
        E = 8
        M = 128
        K = 2
        N_SHARED = 2
        SM = M * N_SHARED
        G = 64
        GE_TEMP = 1.0
        ALPHA = 0.001
        SEQ_AUX = True
        NORM_TOPK = True
        COS_TEMP = 0.78
        CONS_ALPHA = 0.01
        LEAKY_SLOPE = 0.01
        EPS_COS = 1e-08

        def _leaky(x):
            return jnp.where(x >= 0, x, LEAKY_SLOPE * x)

        def _moe_forward(hidden_states, g, wt, wg, w_gate, w_up, w_down, sw_gate, sw_up, sw_down):
            b, s, h = hidden_states.shape
            x = hidden_states.reshape(-1, h)
            T = x.shape[0]
            logits_h = x @ wt.T
            logits_g = g @ wg.T
            logits_g = jnp.repeat(logits_g, s, axis=0)
            logits = (logits_h + logits_g / GE_TEMP) / (1.0 + 1.0 / GE_TEMP)
            scores = jax.nn.softmax(logits, axis=-1)
            topk_w, topk_idx = jax.lax.top_k(scores, K)
            if K > 1 and NORM_TOPK:
                topk_w = topk_w / (topk_w.sum(-1, keepdims=True) + 1e-20)
            onehot = jax.nn.one_hot(topk_idx.reshape(b, s * K), E, dtype=jnp.float32)
            ce = onehot.sum(1) / (s * K / E)
            aux_loss = (ce * scores.reshape(b, s, E).mean(1)).sum(1).mean() * ALPHA
            gp = _leaky(jnp.einsum('th,ehm->etm', x, w_gate))
            up = jnp.einsum('th,ehm->etm', x, w_up)
            y_all = jnp.einsum('etm,emh->eth', gp * up, w_down)
            y_sel = y_all[topk_idx, jnp.arange(T)[:, None], :]
            y = (y_sel * topk_w[..., None]).sum(1).reshape(b, s, h)
            p = _leaky(hidden_states @ sw_gate) * (hidden_states @ sw_up) @ sw_down
            y = y + p
            num = jnp.sum(y * p, -1)
            den = jnp.maximum(jnp.linalg.norm(y, axis=-1), EPS_COS) * jnp.maximum(jnp.linalg.norm(p, axis=-1), EPS_COS)
            closs = CONS_ALPHA * jnp.mean(num / den / (1.0 + COS_TEMP))
            return (y, aux_loss + closs)
        y, _ = _moe_forward(hidden_states, g, wt, wg, w_gate, w_up, w_down, sw_gate, sw_up, sw_down)
        return y

    def _L1_ffn_ref(x, attention_mask, position_ids, router_w, router_b, wq, wk, wv, wo, w1, w2, ln1, ln2):
        import jax, jax.numpy as jnp
        import numpy as np
        B, S, D, H, F = (4, 1024, 256, 16, 1024)
        CAP = 0.125
        ROPE_BASE = 10000.0

        def rmsnorm(x, g):
            return x * jax.lax.rsqrt(jnp.mean(x * x, -1, keepdims=True) + 1e-06) * g

        def rope(t, pos):
            hd = t.shape[-1]
            inv = 1.0 / ROPE_BASE ** (jnp.arange(0, hd, 2, dtype=jnp.float32) / hd)
            f = pos[:, None, :, None].astype(jnp.float32) * inv
            emb = jnp.concatenate([f, f], axis=-1)
            cos, sin = (jnp.cos(emb), jnp.sin(emb))
            rot = jnp.concatenate([-t[..., hd // 2:], t[..., :hd // 2]], axis=-1)
            return t * cos + rot * sin
        b, s, d = x.shape
        hd = d // H
        weights = (x @ router_w)[..., 0] + router_b[0]
        k = int(CAP * s)
        topv, topi = jax.lax.top_k(weights, k)
        thr = topv[:, -1]
        sel_mask = (weights > thr[:, None]).astype(x.dtype)
        kc = k - 1
        sel_idx = jnp.sort(topi[:, :kc], axis=1)
        bidx = jnp.arange(b)[:, None]
        x_sel = x[bidx, sel_idx]
        pos_sel = position_ids[bidx, sel_idx]
        w_sel = weights[bidx, sel_idx]
        m = attention_mask[:, 0]
        m_sel = m[bidx[:, :, None], sel_idx[:, :, None], sel_idx[:, None, :]]
        hn = rmsnorm(x_sel, ln1)

        def heads(t):
            return t.reshape(b, kc, H, hd).transpose(0, 2, 1, 3)
        q = rope(heads(hn @ wq), pos_sel)
        kk = rope(heads(hn @ wk), pos_sel)
        v = heads(hn @ wv)
        sc = jnp.einsum('bhqd,bhkd->bhqk', q, kk) / np.sqrt(hd).astype(np.float32)
        sc = sc + m_sel[:, None]
        a = jax.nn.softmax(sc, axis=-1)
        o = jnp.einsum('bhqk,bhkd->bhqd', a, v).transpose(0, 2, 1, 3).reshape(b, kc, d) @ wo
        x1 = x_sel + o
        x2 = x1 + jax.nn.gelu(rmsnorm(x1, ln2) @ w1) @ w2
        proc = x2 * w_sel[..., None]
        out = jnp.zeros_like(x).at[bidx, sel_idx].set(proc)
        return out + x * (1.0 - sel_mask)[..., None]
    x = x + _L0_attn_ref(_L0_cond_ref(x, mask_BxS_bf1, L0_cond_g_norm, L0_cond_Wq, L0_cond_Wkv, L0_cond_q_scale, L0_cond_k_scale, cond_64, L0_cond_null_attn_bias, L0_cond_w0, L0_cond_b0, L0_cond_g0, L0_cond_w1, L0_cond_b1, L0_cond_g1, L0_cond_w2, L0_cond_b2, L0_cond_Wout, L0_cond_g_out), L0_attn_wq, L0_attn_wk, L0_attn_wv, L0_attn_wo)
    x = x + _L0_ffn_ref(_L0_cond2_ref(x, cond_64, L0_cond2_wt, L0_cond2_wg, L0_cond2_w_gate, L0_cond2_w_up, L0_cond2_w_down, L0_cond2_sw_gate, L0_cond2_sw_up, L0_cond2_sw_down), L0_ffn_w1_w, L0_ffn_w1_s, L0_ffn_w2_w, L0_ffn_w2_s, L0_ffn_h1_w, L0_ffn_h1_s, L0_ffn_h2_w, L0_ffn_h2_s, L0_ffn_w3_w, L0_ffn_w3_s)
    x = x + _L1_attn_ref(_L1_cond_ref(x, fside_16xSxS_0, mask_BxS_bk0, L1_cond_g_in, L1_cond_null_attn_bias, cond_64, L1_cond_Wq, L1_cond_Wkv, L1_cond_Wo, L1_cond_g_out), L1_attn_wq, L1_attn_bq, L1_attn_wk, L1_attn_bk, L1_attn_wv, L1_attn_bv, L1_attn_wo, L1_attn_bo)
    x = x + _L1_ffn_ref(_L1_cond2_ref(x, cond_64, L1_cond2_wt, L1_cond2_wg, L1_cond2_w_gate, L1_cond2_w_up, L1_cond2_w_down, L1_cond2_sw_gate, L1_cond2_sw_up, L1_cond2_sw_down), L1_ffn_attention_mask, L1_ffn_position_ids, L1_ffn_router_w, L1_ffn_router_b, L1_ffn_wq, L1_ffn_wk, L1_ffn_wv, L1_ffn_wo, L1_ffn_w1, L1_ffn_w2, L1_ffn_ln1, L1_ffn_ln2)
    return x

_drawn_inputs = setup_inputs


def setup_inputs(seed=0):
    import zlib

    import numpy as np

    out = dict(_drawn_inputs(seed))
    spreads = {'L0_cond_g_norm': (1.0, 0.2),
     'L0_cond_q_scale': (1.0, 0.2),
     'L0_cond_k_scale': (1.0, 0.2),
     'L0_cond_b0': (0.0, 0.1),
     'L0_cond_g0': (1.0, 0.2),
     'L0_cond_b1': (0.0, 0.1),
     'L0_cond_g1': (1.0, 0.2),
     'L0_cond_b2': (0.0, 0.1),
     'L0_cond_g_out': (1.0, 0.2),
     'L1_cond_g_in': (1.0, 0.2),
     'L1_cond_g_out': (1.0, 0.2),
     'L1_ffn_ln1': (1.0, 0.2),
     'L1_ffn_ln2': (1.0, 0.2)}
    factors = {}
    for name, (base, spread) in spreads.items():
        noise = np.random.default_rng([zlib.crc32(name.encode()), seed]).standard_normal(out[name].shape)
        drawn = base * np.exp(spread * noise) if base else spread * noise
        out[name] = jnp.asarray(drawn.astype(out[name].dtype))
    for name, factor in factors.items():
        out[name] = (out[name] * factor).astype(out[name].dtype)
    return out
```

```python
from contextlib import ExitStack

import numpy as np

import concourse.bass as bass
from concourse import mybir

ALU = mybir.AluOpType
ACT = mybir.ActivationFunctionType
AX = mybir.AxisListType
F32 = mybir.dt.float32
BF16 = mybir.dt.bfloat16
U8 = mybir.dt.uint8
F32R = mybir.dt.float32r
I32 = mybir.dt.int32

P = 128
B = 4
S = 512
NT = S // P
D = 256
DC = D // P
H = 16
DH = 64
INNER = H * DH
MC = INNER // P
NPOS = 640
EPS = 1e-5
NEG = -1e30
THRESH = float(np.float32(0.01))
STAGES = 99


class Sems:

    def __init__(self, ctx, nc, names):
        self.by_name = {n: ctx.enter_context(nc.semaphore(n)) for n in names.split()}
        numbers = [s.num for s in self.by_name.values()]
        self.all = range(min(numbers), max(numbers) + 1)

    def __getitem__(self, name):
        return self.by_name[name]


class Chain:

    def __init__(self, engine, sem):
        self.engine, self.sem, self.n = engine, sem, 0

    def __call__(self, instruction):
        self.n += 1
        instruction.then_inc(self.sem, 1)
        self.engine.wait_ge(self.sem, self.n)


def ln_rows(dve, link, src, st, mv, ve, var_ready, std_ready, n_std, rstd, tiles):
    for t in range(tiles):
        ins = dve.bn_stats(st[:, t, :], src(t))
    link(ins)
    for t in range(tiles):
        ins = dve.bn_aggr(mv[:, t, :], st[:, t, :])
    link(ins)
    dve.tensor_scalar_add(ve[:, 0:tiles], mv[:, 0:tiles, 1], EPS).then_inc(var_ready, 1)
    dve.wait_ge(std_ready, n_std)
    link(dve.reciprocal(rstd[:, 0:tiles], ve[:, 0:tiles]))


def relative_positions(nc, env):
    NP = NPOS // P
    with ExitStack() as ctx:
        sb = lambda n, s, d=F32: ctx.enter_context(nc.sbuf_tensor("rp_" + n, s, d))
        sm = Sems(ctx, nc, "rp_in rp_chain rp_var rp_std rp_norm rp_silu rp_tr rp_ev rp_mm rp_out rp_store")
        w0, b0, g0, b1, g1 = (sb(n, [P, D]) for n in ("w0", "b0", "g0", "b1", "g1"))
        w1 = sb("w1", [P, DC, D])
        w2 = sb("w2", [P, DC, H])
        b2 = sb("b2", [H, 1])
        pos = sb("pos", [P, NP])
        h = sb("h", [P, NP, D])
        hT = sb("hT", [P, DC, NPOS])
        st, mv, ve, rstd = sb("st", [P, NP, 6]), sb("mv", [P, NP, 2]), sb("ve", [P, NP]), sb("rstd", [P, NP])
        tab = sb("tab", [H, NPOS])
        PS = env["PS"]
        a = env["dram"]
        with nc.Block() as block:
            @block.sync
            def _(sp):
                for dst, name in ((w0, "L0_cond_w0"), (b0, "L0_cond_b0"), (g0, "L0_cond_g0"),
                                  (b1, "L0_cond_b1"), (g1, "L0_cond_g1")):
                    row = a[name] if name == "L0_cond_w0" else a[name].unsqueeze(0)
                    sp.dma_start(dst[:, :], row.to_broadcast([P, D])).then_inc(sm["rp_in"], 16)
                sp.dma_start(w1[:, :, :], a["L0_cond_w1"].rearrange("(c p) n -> p c n", p=P)).then_inc(sm["rp_in"], 16)
                sp.dma_start(w2[:, :, :], a["L0_cond_w2"].rearrange("(c p) n -> p c n", p=P)).then_inc(sm["rp_in"], 16)
                sp.dma_start(b2[:, :], a["L0_cond_b2"].unsqueeze(1)).then_inc(sm["rp_in"], 16)
                sp.dma_start(pos[:, :], a["c_pos"]).then_inc(sm["rp_in"], 16)
                sp.wait_ge(sm["rp_out"], 2)
                sp.dma_start(env["rel"], bass.AP(tab, P - 1, [[NPOS, H], [-1, P], [1, S]])).then_inc(sm["rp_store"], 16)
                sp.wait_ge(sm["rp_store"], 16)

            @block.vector
            def _(dve):
                link = Chain(dve, sm["rp_chain"])
                dve.wait_ge(sm["rp_in"], 9 * 16)
                for t in range(NP):
                    ins = dve.scalar_tensor_tensor(out=h[:, t, :], in0=w0[:, :], scalar=pos[:, t:t + 1],
                                                   in1=b0[:, :], op0=ALU.mult, op1=ALU.add)
                link(ins)
                for layer, g in ((0, g0), (1, g1)):
                    ln_rows(dve, link, lambda t: h[:, t, :], st, mv, ve, sm["rp_var"], sm["rp_std"],
                            layer + 1, rstd, NP)
                    for t in range(NP):
                        link(dve.tensor_scalar(h[:, t, :], h[:, t, :], mv[:, t, 0:1], rstd[:, t:t + 1],
                                               ALU.subtract, ALU.mult))
                        dve.tensor_tensor(h[:, t, :], h[:, t, :], g[:, :], ALU.mult).then_inc(sm["rp_norm"], 1)
                    for c in range(DC):
                        dve.wait_ge(sm["rp_tr"], layer * DC + c + 1)
                        dve.tensor_copy(hT[:, c, :], PS[:, 2 * c:2 * c + 2, :].rearrange("p a b -> p (a b)")[:, 0:NPOS])\
                           .then_inc(sm["rp_ev"], 1)
                    if layer == 0:
                        for t in range(NP):
                            dve.wait_ge(sm["rp_mm"], t + 1)
                            link(dve.tensor_tensor(h[:, t, :], PS[:, 4 + t % 2, 0:D], b1[:, :], ALU.add))
                dve.wait_ge(sm["rp_mm"], NP + 1)
                dve.tensor_scalar(tab[:, 0:512], PS[0:H, 4, :], b2[:, 0:1], None, ALU.add).then_inc(sm["rp_out"], 1)
                dve.tensor_scalar(tab[:, 512:NPOS], PS[0:H, 5, 0:NPOS - 512], b2[:, 0:1], None,
                                  ALU.add).then_inc(sm["rp_out"], 1)

            @block.scalar
            def _(act):
                for layer in range(2):
                    act.wait_ge(sm["rp_var"], layer + 1)
                    act.activation(ve[:, :], ve[:, :], ACT.Sqrt).then_inc(sm["rp_std"], 1)
                    for t in range(NP):
                        act.wait_ge(sm["rp_norm"], layer * NP + t + 1)
                        act.activation(h[:, t, :], h[:, t, :], ACT.Silu).then_inc(sm["rp_silu"], 1)

            @block.tensor
            def _(pe):
                for layer in range(2):
                    pe.wait_ge(sm["rp_silu"], (layer + 1) * NP)
                    for c in range(DC):
                        for t in range(NP):
                            ins = pe.transpose(PS[:, 2 * c + t // 4, t % 4 * P:t % 4 * P + P],
                                               h[:, t, c * P:c * P + P], env["ident"])
                        ins.then_inc(sm["rp_tr"], 1)
                    pe.wait_ge(sm["rp_ev"], (layer + 1) * DC)
                    if layer == 0:
                        for t in range(NP):
                            if t >= 2:
                                pe.wait_ge(sm["rp_chain"], 4 + NP + t - 1)
                            for c in range(DC):
                                ins = pe.matmul(PS[:, 4 + t % 2, 0:D], hT[:, c, t * P:t * P + P], w1[:, c, :],
                                                start=(c == 0), stop=(c == DC - 1))
                            ins.then_inc(sm["rp_mm"], 1)
                    else:
                        for n, (lo, hi) in enumerate(((0, 512), (512, NPOS))):
                            for c in range(DC):
                                ins = pe.matmul(PS[0:H, 4 + n, 0:hi - lo], w2[:, c, :], hT[:, c, lo:hi],
                                                start=(c == 0), stop=(c == DC - 1))
                        ins.then_inc(sm["rp_mm"], 1)
        nc.all_engine_barrier(sems_to_clear=sm.all)


def cond_attention_weights(nc, env, ctx, layer):
    L0 = layer == 0
    pre = f"L{layer}_cond_"
    a = env["dram"]
    sb = lambda n, s, d=F32: ctx.enter_context(nc.sbuf_tensor(f"ca{layer}_" + n, s, d))
    w = {
        "wq": sb("wq", [P, DC, INNER]), "wkk": sb("wkk", [P, DC, P]), "wv": sb("wv", [P, DC, DH]),
        "wo": sb("wo", [P, MC, D]), "g_in": sb("g_in", [P, DC]), "g_out": sb("g_out", [P, DC]),
        "kn": sb("kn", [P, 1]), "vn": sb("vn", [P, 1]), "knh": sb("knh", [P, MC * H]),
        "vnb": sb("vnb", [P, MC * H]), "vw": sb("vw", [H, D]), "nb": sb("nb", [P, H]),
        "sc": sb("sc", [P, 4]), "qk": sb("qk", [P, 2]),
    }
    PS = env["PS"]
    with ExitStack() as inner:
        sm = Sems(inner, nc, "cw_in cw_chain cw_mm cw_std")
        with nc.Block() as block:
            @block.sync
            def _(sp):
                def load(dst, src):
                    sp.dma_start(dst, src).then_inc(sm["cw_in"], 16)

                load(w["wq"][:, :, :], a[pre + "Wq"].rearrange("(c p) n -> p c n", p=P))
                wkv = a[pre + "Wkv"].rearrange("(c p) n -> p c n", p=P)
                for half in range(2):
                    load(w["wkk"][:, :, half * DH:half * DH + DH], wkv[:, :, 0:DH])
                load(w["wv"][:, :, :], wkv[:, :, DH:2 * DH])
                load(w["wo"][:, :, :], a[pre + ("Wout" if L0 else "Wo")].rearrange("(c p) n -> p c n", p=P))
                load(w["g_in"][:, :], a[pre + ("g_norm" if L0 else "g_in")])
                load(w["g_out"][:, :], a[pre + "g_out"])
                for half in range(2):
                    part = slice(half * DH, half * DH + DH)
                    load(w["kn"][part, :], a["cond_64"][0:1, :].rearrange("o d -> d o"))
                    load(w["vn"][part, :], a["cond_64"][1:2, :].rearrange("o d -> d o"))
                    if L0:
                        load(w["qk"][part, 0:1], a[pre + "q_scale"].unsqueeze(1))
                        load(w["qk"][part, 1:2], a[pre + "k_scale"].unsqueeze(1))
                load(w["nb"][:, :], a[pre + "null_attn_bias"].unsqueeze(0).to_broadcast([P, H]))

            @block.vector
            def _(dve):
                link = Chain(dve, sm["cw_chain"])
                dve.wait_ge(sm["cw_in"], 16 * (16 if L0 else 12))
                link(dve.memset(w["knh"][:, :], 0.0))
                link(dve.memset(w["vnb"][:, :], 0.0))
                link(dve.tensor_scalar(w["nb"][:, :], w["nb"][:, :], -1.0, None, ALU.mult))
                if L0:
                    link(dve.tensor_tensor(w["sc"][:, 0:1], w["qk"][:, 0:1], w["qk"][:, 1:2], ALU.mult))
                    link(dve.tensor_scalar(w["sc"][:, 0:1], w["sc"][:, 0:1], 8.0, None, ALU.mult))
                    link(dve.tensor_tensor(w["sc"][:, 1:2], w["kn"][:, :], w["kn"][:, :], ALU.mult))
                    dve.wait_ge(sm["cw_std"], 1)
                    link(dve.tensor_scalar(w["sc"][:, 2:3], w["sc"][:, 2:3], 1e-12, None, ALU.max))
                    link(dve.reciprocal(w["sc"][:, 3:4], w["sc"][:, 2:3]))
                    link(dve.tensor_scalar(w["kn"][:, :], w["kn"][:, :], w["sc"][:, 3:4], w["sc"][:, 0:1],
                                           ALU.mult, ALU.mult))
                else:
                    link(dve.tensor_scalar(w["kn"][:, :], w["kn"][:, :], DH ** -0.5, None, ALU.mult))
                for half in range(2):
                    part = slice(half * DH, half * DH + DH)
                    dve.tensor_copy(w["knh"][part, half:MC * H:H + 2], w["kn"][part, :].to_broadcast([DH, MC]))
                    ins = dve.tensor_copy(w["vnb"][part, half:MC * H:H + 2],
                                          w["vn"][part, :].to_broadcast([DH, MC]))
                link(ins)
                dve.wait_ge(sm["cw_mm"], 2 if L0 else 1)
                link(dve.tensor_copy(w["vw"][:, :], PS[0:H, 1, 0:D]))

            @block.scalar
            def _(act):
                if L0:
                    act.wait_ge(sm["cw_mm"], 1)
                    act.activation(w["sc"][:, 2:3], PS[:, 0, 0:1], ACT.Sqrt).then_inc(sm["cw_std"], 1)

            @block.tensor
            def _(pe):
                if L0:
                    pe.wait_ge(sm["cw_chain"], 6)
                    pe.matmul(PS[:, 0, 0:1], env["half_ones"], w["sc"][:, 1:2], start=True,
                              stop=True).then_inc(sm["cw_mm"], 1)
                pe.wait_ge(sm["cw_chain"], 10 if L0 else 5)
                for m in range(MC):
                    ins = pe.matmul(PS[0:H, 1, 0:D], w["vnb"][:, m * H:m * H + H], w["wo"][:, m, :],
                                    start=(m == 0), stop=(m == MC - 1))
                ins.then_inc(sm["cw_mm"], 1)
        nc.all_engine_barrier(sems_to_clear=sm.all)
    return w


COND_SEMS = ("ca_nul ca_nhi ca_nlo ca_masks ca_qhi ca_qlo ca_khi ca_klo ca_in ca_bias0 ca_bias1 ca_chain ca_mask ca_var ca_std ca_xn ca_xT ca_xnT ca_k ca_kcp ca_ksq ca_kss ca_knrm "
             "ca_kT ca_v ca_vcp ca_q ca_qcp ca_qsq ca_ss ca_nrm ca_rn ca_bc ca_qsc ca_sn ca_sneg ca_S ca_tt ca_exp "
             "ca_tr ca_evd ca_eva ca_av ca_pd ca_pn ca_Oev ca_OTt ca_OTd ca_OTa ca_cT ca_out ca_hn ca_hTt ca_hT")


def cond_attention(nc, env, sm, w, b, layer):
    L0 = layer == 0
    X, PS, ident, a = env["X"], env["PS"], env["ident"], env["dram"]
    NU = H * NT
    with ExitStack() as ctx:
        sb = lambda n, s, d=F32: ctx.enter_context(nc.sbuf_tensor(f"cb{layer}_" + n, s, d))
        m8, mb = sb("m8", [P, S], U8), sb("mb", [P, NT, S], BF16)
        st, mv, ve, rstd = sb("st", [P, NT, 6]), sb("mv", [P, NT, 2]), sb("ve", [P, NT]), sb("rstd", [P, NT])
        xn = sb("xn", [P, NT, D])
        QT, kT, V = sb("QT", [P, MC, S]), sb("kT", [P, S]), sb("V", [P, NT, DH])
        Q2, kh, kl = sb("Q2", [P, H, S], F32R), sb("kh", [P, S], F32R), sb("kl", [P, S], F32R)
        sneg, nm, rs, pn = (sb(n, [P, NT, H]) for n in ("sneg", "nm", "rs", "pn"))
        rden, cpn = sb("rden", [P, NT, H]), sb("cpn", [P, NT, H])
        sc, pr, pt = sb("sc", [P, 3, S]), sb("pr", [P, 3, S]), sb("pt", [P, 3, S])
        O, OT, cT = sb("O", [P, NT, INNER]), QT, sb("cT", [H, S])
        xnT = pt[:, 1:3]
        hT = lambda c: (env["hTs"][:, bass.ds(b * DC + c, 1), :].rearrange("p o k -> p (o k)") if L0
                        else env["hT"][:, c, :])
        nul = sb("nul", [H, S])
        if L0:
            kr, knrm, qsq, ksq, nrm = sc[:, 0], sc[:, 1], pr[:, 0:2], pt[:, 0], cT
            toep = sb("toep", [P, H, S])
            nhi, nlo = sb("nhi", [H, S], F32R), sb("nlo", [H, S], F32R)
        else:
            bias = sb("bias", [P, 2, NT, S])
        xt = lambda t: X[:, bass.ds(b * NT + t, 1), :].rearrange("p o d -> p (o d)")
        on_dve = lambda u: u % NT >= 2
        evs = lambda t: (sm["ca_evd"], 2) if t >= 2 else (sm["ca_eva"], 2)

        def wait_ev(eng, u):
            h, t = divmod(u, NT)
            eng.wait_ge(sm["ca_evd"] if t >= 2 else sm["ca_eva"], 2 * h + t % 2 + 1)

        width = lambda t: P * (t + 1)

        with nc.Block() as block:
            @block.sync
            def _(sp):
                sp.dma_start(m8[:, :], a["mask_BxS_bf1" if L0 else "mask_BxS_bk0"][bass.ds(b, 1), :]
                             .to_broadcast([P, S])).then_inc(sm["ca_in"], 16)
                if L0:
                    sp.dma_start(toep[:, :, :], env["rel"].rearrange("h p c -> p h c")).then_inc(sm["ca_bias0"], 16)
                else:
                    for h in range(H):
                        if h >= 2:
                            sp.wait_ge(sm["ca_tt"], NT * (h - 1))
                        for t in range(NT):
                            sp.dma_start(bias[:, h % 2, t, 0:width(t)],
                                         a["fside_16xSxS_0"][h, t * P:t * P + P, 0:width(t)])\
                              .then_inc(sm[f"ca_bias{h % 2}"], 16)

            @block.vector
            def _(dve):
                link = Chain(dve, sm["ca_chain"])
                ln_rows(dve, link, xt, st, mv, ve, sm["ca_var"], sm["ca_std"], 1, rstd, NT)
                for t in range(NT):
                    dve.tensor_scalar(xn[:, t, :], xt(t), mv[:, t, 0:1], rstd[:, t:t + 1],
                                      ALU.subtract, ALU.mult).then_inc(sm["ca_xn"], 1)
                for c in range(DC):
                    dve.wait_ge(sm["ca_xT"], c + 1)
                    dve.tensor_scalar(xnT[:, c, :], PS[:, c, :], w["g_in"][:, c:c + 1], None,
                                      ALU.mult).then_inc(sm["ca_xnT"], 1)
                dve.wait_ge(sm["ca_k"], 1)
                if L0:
                    dve.tensor_copy(kr[:, :], PS[:, 4, :]).then_inc(sm["ca_kcp"], 1)
                else:
                    dve.tensor_scalar(kT[:, :], PS[:, 4, :], DH ** -0.5, None, ALU.mult).then_inc(sm["ca_kT"], 1)
                dve.wait_ge(sm["ca_v"], 1)
                dve.tensor_copy(V[:, :, :], PS[:, 5, 0:NT * DH].rearrange("p (t d) -> p t d", t=NT))\
                   .then_inc(sm["ca_vcp"], 1)
                for m in range(MC):
                    dve.wait_ge(sm["ca_q"], m + 1)
                    dve.tensor_copy(QT[:, m, :], PS[:, 2 + m % 2, :]).then_inc(sm["ca_qcp"], 1)
                    if L0 and m == 2:
                        dve.wait_ge(sm["ca_knrm"], 1)
                        link(dve.tensor_scalar(knrm[:, :], knrm[:, :], 1e-12, None, ALU.max))
                        link(dve.reciprocal(ksq[:, :], knrm[:, :]))
                        dve.scalar_tensor_tensor(out=kT[:, :], in0=kr[:, :], scalar=w["sc"][:, 0:1], in1=ksq[:, :],
                                                 op0=ALU.mult, op1=ALU.mult).then_inc(sm["ca_kT"], 1)
                if L0:
                    dve.wait_ge(sm["ca_nrm"], 1)
                    link(dve.tensor_scalar(nrm[:, :], nrm[:, :], 1e-12, None, ALU.max))
                    dve.reciprocal(nrm[:, :], nrm[:, :]).then_inc(sm["ca_rn"], 1)
                    dve.wait_ge(sm["ca_rn"], 1)
                    dve.tensor_copy(nhi[:, :], nrm[:, :]).then_inc(sm["ca_nhi"], 1)
                    dve.wait_ge(sm["ca_nhi"], 1)
                    dve.tensor_tensor(nlo[:, :], nrm[:, :], nhi[:, :].bitcast(F32), ALU.subtract).then_inc(sm["ca_nlo"], 1)
                    dve.wait_ge(sm["ca_sn"], 1)
                    dve.tensor_tensor(nul[:, :], nrm[:, :], PS[0:H, 0, :], ALU.mult).then_inc(sm["ca_nul"], 1)
                    for m in range(MC):
                        dve.wait_ge(sm["ca_bc"], m + 1)
                        dve.tensor_tensor(QT[:, m, :], QT[:, m, :], PS[:, 2 + m % 2, :],
                                          ALU.mult).then_inc(sm["ca_qsc"], 1)
                else:
                    dve.wait_ge(sm["ca_sn"], 1)
                    dve.tensor_copy(nul[:, :], PS[0:H, 0, :]).then_inc(sm["ca_nul"], 1)
                dve.wait_ge(sm["ca_sn"], 2)
                dve.scalar_tensor_tensor(out=sneg[:, :, :], in0=PS[:, 6, 0:NT * H].rearrange("p (t h) -> p t h", t=NT),
                                         scalar=-1.0, in1=w["nb"][:, :].unsqueeze(1).to_broadcast([P, NT, H]),
                                         op0=ALU.mult, op1=ALU.add).then_inc(sm["ca_sneg"], 1)
                dve.wait_ge(sm["ca_sneg"], 1)

                def biased(u):
                    h, t = divmod(u, NT)
                    n = width(t)
                    dve.wait_ge(sm["ca_S"], u + 1)
                    if u >= 3:
                        dve.wait_ge(sm["ca_exp"], u - 2)
                    if L0:
                        dve.wait_ge(sm["ca_bias0"], 16)
                        bb = toep[:, h, S - n:S]
                    else:
                        dve.wait_ge(sm[f"ca_bias{h % 2}"], 16 * NT * (h // 2 + 1))
                        bb = bias[:, h % 2, t, 0:n]
                    dve.tensor_tensor_reduce(out=sc[:, u % 3, 0:n], in0=PS[:, u % 3, 0:n], in1=bb, scale=-1.0,
                                             scalar=sneg[:, t, h:h + 1], op0=ALU.add, op1=ALU.min,
                                             accum_out=nm[:, t, h:h + 1]).then_inc(sm["ca_tt"], 1)

                def move(u):
                    t = u % NT
                    dve.wait_ge(sm["ca_tr"], u + 1)
                    if u >= 3:
                        dve.wait_ge(sm["ca_av"], u - 2)
                    dve.tensor_copy(pt[:, u % 3, 0:width(t)], PS[:, 3 + u % 3, 0:width(t)]).then_inc(sm["ca_evd"], 1)

                def null_difference(g):
                    hs = slice(4 * g, 4 * g + 4)
                    dve.wait_ge(sm["ca_tt"], 16 * (g + 1))
                    dve.tensor_tensor(pn[:, :, hs], nm[:, :, hs], sneg[:, :, hs],
                                      ALU.subtract).then_inc(sm["ca_pd"], 1)

                def normalise(g):
                    hs = slice(4 * g, 4 * g + 4)
                    dve.wait_ge(sm["ca_pn"], g + 1)
                    dve.wait_ge(sm["ca_exp"], 16 * (g + 1))
                    link(dve.tensor_tensor(rden[:, :, hs], rs[:, :, hs], pn[:, :, hs], ALU.add))
                    link(dve.reciprocal(rden[:, :, hs], rden[:, :, hs]))
                    link(dve.tensor_tensor(cpn[:, :, hs], rden[:, :, hs], pn[:, :, hs], ALU.mult))
                    dve.wait_ge(sm["ca_av"], 16 * (g + 1))
                    for k in range(2):
                        ins = dve.tensor_tensor(
                            O[:, 2 * k:2 * k + 2, g * D:(g + 1) * D].rearrange("p t (h d) -> p t h d", d=DH),
                            PS[:, 6 + k, :].rearrange("p (t h d) -> p t h d", t=2, d=DH),
                            rden[:, 2 * k:2 * k + 2, hs].unsqueeze(3).to_broadcast([P, 2, 4, DH]), ALU.mult)
                    ins.then_inc(sm["ca_Oev"], 1)

                for u in range(NU + 4):
                    if u < NU:
                        biased(u)
                    if 2 <= u < NU + 2 and on_dve(u - 2):
                        move(u - 2)
                    if u % 16 == 0 and u:
                        null_difference(u // 16 - 1)
                    if u % 16 == 3 and u > 16:
                        normalise(u // 16 - 1)
                for m in range(0, MC, 2):
                    dve.wait_ge(sm["ca_OTt"], m + 1)
                    dve.tensor_copy(OT[:, m, :], PS[:, m % 2, :]).then_inc(sm["ca_OTd"], 1)
                dve.wait_ge(sm["ca_OTt"], MC + 1)
                dve.tensor_copy(cT[:, :], PS[0:H, 2, :]).then_inc(sm["ca_cT"], 1)
                dve.wait_ge(sm["ca_out"], NT)
                row = lambda t: PS[:, 4 + t // 2, t % 2 * D:t % 2 * D + D]
                ln_rows(dve, link, row, st, mv, ve, sm["ca_var"], sm["ca_std"], 2, rstd, NT)
                for t in range(NT):
                    dve.tensor_scalar(xn[:, t, :], row(t), mv[:, t, 0:1], rstd[:, t:t + 1],
                                      ALU.subtract, ALU.mult).then_inc(sm["ca_hn"], 1)
                for c in range(DC):
                    dve.wait_ge(sm["ca_hTt"], c + 1)
                    dve.tensor_scalar(hT(c), PS[:, 6 + c, :], w["g_out"][:, c:c + 1], None,
                                      ALU.mult).then_inc(sm["ca_hT"], 1)

            @block.gpsimd
            def _(pool):
                pool.wait_ge(sm["ca_in"], 16)
                for t in range(NT):
                    pool.tensor_scalar(mb[:, t, 0:width(t)], m8[:, 0:width(t)], 0.0, NEG, ALU.is_equal,
                                       ALU.mult).then_inc(sm["ca_mask"], 1)
                for t in range(NT):
                    pool.wait_ge(sm["ca_mask"], NT)
                    last = mb[:, t, t * P:t * P + P]
                    pool.tensor_tensor(last, last, env["causal_bf"], ALU.add).then_inc(sm["ca_masks"], 1)
                pool.wait_ge(sm["ca_kT"], 1)
                pool.tensor_copy(kh[:, :], kT[:, :]).then_inc(sm["ca_khi"], 1)
                pool.wait_ge(sm["ca_khi"], 1)
                pool.tensor_tensor(kl[:, :], kT[:, :], kh[:, :].bitcast(F32), ALU.subtract).then_inc(sm["ca_klo"], 1)
                for h in range(H):
                    if h:
                        pool.wait_ge(sm["ca_qlo"], h)
                    else:
                        pool.wait_ge(sm["ca_klo"], 1)
                    pool.wait_ge(sm["ca_qhi"], h + 1)
                    part = slice(h % 2 * DH, h % 2 * DH + DH)
                    other = slice((h + 1) % 2 * DH, (h + 1) % 2 * DH + DH)
                    pool.tensor_tensor(Q2[other, h, :], QT[part, h // 2, :], Q2[part, h, :].bitcast(F32),
                                       ALU.subtract).then_inc(sm["ca_qlo"], 1)

            @block.scalar
            def _(act):
                act.wait_ge(sm["ca_var"], 1)
                act.activation(ve[:, :], ve[:, :], ACT.Sqrt).then_inc(sm["ca_std"], 1)
                if L0:
                    act.wait_ge(sm["ca_kcp"], 1)
                    act.activation(ksq[:, :], kr[:, :], ACT.Square).then_inc(sm["ca_ksq"], 1)
                    act.wait_ge(sm["ca_kss"], 1)
                    act.activation(knrm[:, :], PS[:, 7, :], ACT.Sqrt).then_inc(sm["ca_knrm"], 1)
                    for m in range(MC):
                        act.wait_ge(sm["ca_qcp"], m + 1)
                        if m >= 2:
                            act.wait_ge(sm["ca_ss"], m - 1)
                        act.activation(qsq[:, m % 2, :], QT[:, m, :], ACT.Square).then_inc(sm["ca_qsq"], 1)
                    act.wait_ge(sm["ca_ss"], MC)
                    act.activation(nrm[:, :], PS[0:H, 6, :], ACT.Sqrt).then_inc(sm["ca_nrm"], 1)

                for h in range(H):
                    if h % 2 == 0:
                        act.wait_ge(sm["ca_qsc" if L0 else "ca_qcp"], h // 2 + 1)
                    part = slice(h % 2 * DH, h % 2 * DH + DH)
                    act.activation(Q2[part, h, :], QT[part, h // 2, :], ACT.Copy).then_inc(sm["ca_qhi"], 1)

                def exponential(u):
                    h, t = divmod(u, NT)
                    n = width(t)
                    act.wait_ge(sm["ca_tt"], u + 1)
                    if u >= 3:
                        act.wait_ge(sm["ca_tr"], u - 2)
                    act.activation(pr[:, u % 3, 0:n], sc[:, u % 3, 0:n], ACT.Exp, bias=nm[:, t, h:h + 1], scale=-1.0,
                                   accum_out=rs[:, t, h:h + 1]).then_inc(sm["ca_exp"], 1)

                def move(u):
                    t = u % NT
                    act.wait_ge(sm["ca_tr"], u + 1)
                    if u >= 3:
                        act.wait_ge(sm["ca_av"], u - 2)
                    act.activation(pt[:, u % 3, 0:width(t)], PS[:, 3 + u % 3, 0:width(t)],
                                   ACT.Copy).then_inc(sm["ca_eva"], 1)

                for u in range(NU + 4):
                    if u < NU:
                        exponential(u)
                    if 2 <= u < NU + 2 and not on_dve(u - 2):
                        move(u - 2)
                    if u % 16 == 0 and u:
                        g = u // 16 - 1
                        act.wait_ge(sm["ca_pd"], g + 1)
                        act.activation(pn[:, :, 4 * g:4 * g + 4], pn[:, :, 4 * g:4 * g + 4],
                                       ACT.Exp).then_inc(sm["ca_pn"], 1)
                for m in range(1, MC, 2):
                    act.wait_ge(sm["ca_OTt"], m + 1)
                    act.activation(OT[:, m, :], PS[:, m % 2, :], ACT.Copy).then_inc(sm["ca_OTa"], 1)
                act.wait_ge(sm["ca_var"], 2)
                act.activation(ve[:, :], ve[:, :], ACT.Sqrt).then_inc(sm["ca_std"], 1)

            @block.tensor
            def _(pe):
                for c in range(DC):
                    for t in range(NT):
                        if c == 0:
                            pe.wait_ge(sm["ca_xn"], t + 1)
                        ins = pe.transpose(PS[:, c, t * P:t * P + P], xn[:, t, c * P:c * P + P], ident)
                    ins.then_inc(sm["ca_xT"], 1)
                pe.wait_ge(sm["ca_xnT"], DC)
                for c in range(DC):
                    ins = pe.matmul(PS[:, 4, :], w["wkk"][:, c, :], xnT[:, c, :], start=(c == 0), stop=(c == DC - 1))
                ins.then_inc(sm["ca_k"], 1)
                for t in range(NT):
                    for c in range(DC):
                        ins = pe.matmul(PS[:, 5, t * DH:t * DH + DH], xnT[:, c, t * P:t * P + P], w["wv"][:, c, :],
                                        start=(c == 0), stop=(c == DC - 1))
                ins.then_inc(sm["ca_v"], 1)
                for m in range(MC + 2):
                    if m < MC:
                        if m >= 2:
                            pe.wait_ge(sm["ca_qcp"], m - 1)
                        for c in range(DC):
                            ins = pe.matmul(PS[:, 2 + m % 2, :], w["wq"][:, c, m * P:m * P + P], xnT[:, c, :],
                                            start=(c == 0), stop=(c == DC - 1))
                        ins.then_inc(sm["ca_q"], 1)
                    if 1 <= m <= MC:
                        pe.wait_ge(sm["ca_qcp"], m)
                        ins = pe.matmul(PS[0:H, 0, :], w["knh"][:, (m - 1) * H:m * H], QT[:, m - 1, :], start=(m == 1),
                                        stop=(m == MC))
                        if m == MC:
                            ins.then_inc(sm["ca_sn"], 1)
                    if L0 and m == 0:
                        pe.wait_ge(sm["ca_ksq"], 1)
                        pe.matmul(PS[:, 7, :], env["half_ones"], ksq[:, :], start=True, stop=True)\
                          .then_inc(sm["ca_kss"], 1)
                    if L0 and m >= 2:
                        pe.wait_ge(sm["ca_qsq"], m - 1)
                        pe.matmul(PS[0:H, 6, :], env["head_of"][:, m - 2, :], qsq[:, m % 2, :], start=(m == 2),
                                  stop=(m == MC + 1)).then_inc(sm["ca_ss"], 1)

                def null_turn():
                    pe.wait_ge(sm["ca_nul"], 1)
                    for t in range(NT):
                        ins = pe.transpose(PS[:, 6, t * H:t * H + H], nul[:, t * P:t * P + P], ident[0:H, 0:H])
                    ins.then_inc(sm["ca_sn"], 1)

                if L0:
                    pe.wait_ge(sm["ca_nhi"], 1)
                    pe.wait_ge(sm["ca_nlo"], 1)
                    for m in range(MC):
                        if m >= 2:
                            pe.wait_ge(sm["ca_qsc"], m - 1)
                        pe.matmul(PS[:, 2 + m % 2, :], env["of_head"][:, m, :], nhi[:, :], start=True, stop=False)
                        pe.matmul(PS[:, 2 + m % 2, :], env["of_head"][:, m, :], nlo[:, :], start=False,
                                  stop=True).then_inc(sm["ca_bc"], 1)
                        if m == 1:
                            null_turn()
                    pe.wait_ge(sm["ca_qsc"], MC)
                else:
                    null_turn()
                pe.wait_ge(sm["ca_khi"], 1)
                pe.wait_ge(sm["ca_klo"], 1)
                pe.wait_ge(sm["ca_masks"], NT)
                pe.wait_ge(sm["ca_vcp"], 1)
                pe.wait_ge(sm["ca_sneg"], 1)

                def scores(u):
                    h, t = divmod(u, NT)
                    n = width(t)
                    if t == 0:
                        pe.wait_ge(sm["ca_qhi"], h + 1)
                        pe.wait_ge(sm["ca_qlo"], h + 1)
                    if u >= 3:
                        pe.wait_ge(sm["ca_tt"], u - 2)
                    pe.matmul(PS[:, u % 3, 0:n], env["ident_bf"], mb[:, t, 0:n], start=True, stop=False)
                    pe.matmul(PS[:, u % 3, 0:n], Q2[:, h, t * P:t * P + P], kl[:, 0:n], start=False, stop=False)
                    pe.matmul(PS[:, u % 3, 0:n], Q2[:, h, t * P:t * P + P], kh[:, 0:n], start=False,
                              stop=True).then_inc(sm["ca_S"], 1)

                def turn(u):
                    t = u % NT
                    pe.wait_ge(sm["ca_exp"], u + 1)
                    if u >= 3:
                        wait_ev(pe, u - 3)
                    for j in range(t + 1):
                        ins = pe.transpose(PS[:, 3 + u % 3, j * P:j * P + P], pr[:, u % 3, j * P:j * P + P], ident)
                    ins.then_inc(sm["ca_tr"], 1)

                def values(u):
                    h, t = divmod(u, NT)
                    wait_ev(pe, u)
                    if u % 16 == 0 and u:
                        pe.wait_ge(sm["ca_Oev"], u // 16)
                    o = t % 2 * D + h % 4 * DH
                    for j in range(t + 1):
                        ins = pe.matmul(PS[:, 6 + t // 2, o:o + DH], pt[:, u % 3, j * P:j * P + P], V[:, j, :],
                                        start=(j == 0), stop=(j == t))
                    ins.then_inc(sm["ca_av"], 1)

                def late(v):
                    return v > 0 and v % 16 == 0

                for u in range(NU + 4):
                    if u < NU:
                        scores(u)
                    v = u - 4
                    if late(v - 1):
                        values(v - 1)
                    if v >= 0 and not late(v):
                        values(v)
                    if 2 <= u < NU + 2:
                        turn(u - 2)
                pe.wait_ge(sm["ca_Oev"], 4)
                for m in range(MC):
                    if m >= 2:
                        pe.wait_ge(sm["ca_OTa" if m % 2 else "ca_OTd"], m // 2)
                    for t in range(NT):
                        ins = pe.transpose(PS[:, m % 2, t * P:t * P + P], O[:, t, m * P:m * P + P], ident)
                    ins.then_inc(sm["ca_OTt"], 1)
                for t in range(NT):
                    ins = pe.transpose(PS[0:H, 2, t * P:t * P + P], cpn[:, t, :], ident)
                ins.then_inc(sm["ca_OTt"], 1)
                pe.wait_ge(sm["ca_OTd"], MC // 2)
                pe.wait_ge(sm["ca_OTa"], MC // 2)
                pe.wait_ge(sm["ca_cT"], 1)
                for t in range(NT):
                    o = PS[:, 4 + t // 2, t % 2 * D:t % 2 * D + D]
                    for m in range(MC):
                        pe.matmul(o, OT[:, m, t * P:t * P + P], w["wo"][:, m, :], start=(m == 0), stop=False)
                    pe.matmul(o, cT[:, t * P:t * P + P], w["vw"][:, :], start=False,
                              stop=True).then_inc(sm["ca_out"], 1)
                pe.wait_ge(sm["ca_hn"], NT)
                for c in range(DC):
                    for t in range(NT):
                        ins = pe.transpose(PS[:, 6 + c, t * P:t * P + P], xn[:, t, c * P:c * P + P], ident)
                    ins.then_inc(sm["ca_hTt"], 1)
        nc.all_engine_barrier(sems_to_clear=sm.all)


AD = D // H
HC = 4
NB = S // 64
GH = 2
NG = H // GH
GR = NT * GH * NB


def gated_attention_weights(nc, env, ctx):
    a, names = env["dram"], ("wq", "wk", "wv", "wo")
    sb = lambda n, s, d=F32: ctx.enter_context(nc.sbuf_tensor("ga_" + n, s, d))
    w = {"wq": sb("wq", [P, DC, HC * P]), "wk": sb("wk", [P, DC, HC * P]), "wv": sb("wv", [P, DC, D]),
         "wo": sb("wo", [P, DC, D]), "blocks": sb("blocks", [NB, S]), "key_rows": sb("key_rows", [NB, P]),
         "blocks_bf": sb("blocks_bf", [NB, S], BF16), "key_rows_bf": sb("key_rows_bf", [NB, P], BF16),
         "head4": sb("head4", [P, HC, H]), "pick": sb("pick", [GR, GH * NT, P], BF16), "tile_of": sb("tile_of", [GR, NT]),
         "own_block": sb("own_block", [P, NT, NB]), "eye8": sb("eye8", [NB, NB]),
         "spread": sb("spread", [P, 4, HC, P], F32R)}
    with ExitStack() as inner:
        raw = {n: inner.enter_context(nc.sbuf_tensor("ga_raw" + n, [P, DC, D], F32)) for n in ("wq", "wk")}
        spread = inner.enter_context(nc.sbuf_tensor("ga_rawspread", [P, 4, HC, P], F32))
        pick = inner.enter_context(nc.sbuf_tensor("ga_rawpick", [GR, GH * NT, P], F32))
        sm = Sems(inner, nc, "gw_in gw_zero gw_spread")
        with nc.Block() as block:
            @block.sync
            def _(sp):
                for n in names:
                    dst = raw[n] if n in raw else w[n]
                    sp.dma_start(dst[:, :, :], a["L0_attn_" + n].rearrange("(c p) n -> p c n", p=P))\
                      .then_inc(sm["gw_in"], 16)
                for n in ("blocks", "key_rows", "tile_of", "eye8"):
                    sp.dma_start(w[n][:, :], a["c_" + n]).then_inc(sm["gw_in"], 16)
                for n in ("head4", "own_block"):
                    sp.dma_start(w[n][:, :, :], a["c_" + n]).then_inc(sm["gw_in"], 16)
                sp.dma_start(pick[:, :, :], a["c_pick"]).then_inc(sm["gw_in"], 16)
                sp.dma_start(spread[:, :, :, :], a["c_spread"]).then_inc(sm["gw_in"], 16)

            @block.vector
            def _(dve):
                for n in raw:
                    dve.memset(w[n][:, :, :], 0.0).then_inc(sm["gw_zero"], 1)
                dve.wait_ge(sm["gw_zero"], 2)
                dve.wait_ge(sm["gw_in"], 12 * 16)
                dve.tensor_copy(w["pick"][:, :, :], pick[:, :, :]).then_inc(sm["gw_spread"], 1)
                dve.tensor_copy(w["spread"][:, :, :, :], spread[:, :, :, :]).then_inc(sm["gw_spread"], 1)
                for n in ("blocks", "key_rows"):
                    dve.tensor_copy(w[n + "_bf"][:, :], w[n][:, :]).then_inc(sm["gw_spread"], 1)
                for n in raw:
                    for c in range(DC):
                        dve.tensor_copy(w[n][:, c, :].rearrange("p (h d) -> p h d", d=32)[:, :, 0:AD],
                                        raw[n][:, c, :].rearrange("p (h d) -> p h d", d=AD)).then_inc(sm["gw_spread"], 1)
                dve.wait_ge(sm["gw_spread"], 8)
        nc.all_engine_barrier(sems_to_clear=sm.all)
    return w


GATED_SEMS = ("ga_oT ga_back ga_hT ga_hi ga_lo ga_sp ga_pd ga_pa ga_chain ga_zero ga_sum ga_qm ga_qmcp ga_kd ga_bs ga_gate ga_qk ga_qkcp ga_md ga_mdcp ga_v ga_vcp ga_prod "
              "ga_sd ga_sde ga_S ga_neg ga_exp ga_g1 ga_g2 ga_aa ga_aT ga_D ga_keep ga_kcp ga_T ga_ev ga_av ga_cd ga_cdv "
              "ga_Oev ga_OT ga_OTcp ga_out ga_x")


def gated_attention(nc, env, sm, w, b):
    X, PS, ident = env["X"], env["PS"], env["ident"]
    with ExitStack() as ctx:
        sb = lambda n, s, d=F32: ctx.enter_context(nc.sbuf_tensor("gb_" + n, s, d))
        hm, qm, kd = sb("hm", [P, DC, NB]), sb("qm", [P, HC, NB]), sb("kd", [P, HC, P])
        gate_bf = sb("gate_bf", [NB, HC * P], BF16)
        OR = 32 + AD
        oT = sb("oT", [OR, S])
        gate = oT[0:NB, :]
        gd, gdiag = sb("gd", [NB, H, NB]), sb("gdiag", [NB, H])
        qk = sb("qk", [P, 2, 2, S])
        hi, lo, parts = sb("hi", [P, 2, S], F32R), sb("lo", [P, 2, S], F32R), sb("parts", [P, 2, H, S], F32R)
        masked, sd = sb("masked", [P, NT, H]), sb("sd", [P, NT, H])
        bmax = sb("bmax", [P, NT, H, NB + 1])
        nm, rs, edf, rden, cd, tmp = (sb(n, [P, NT, H]) for n in ("nm", "rs", "edf", "rden", "cd", "tmp"))
        open_, kdg = sb("open", [P, NT, H]), sb("kdg", [P, NT, GH])
        aa, kq, sel = sb("aa", [P, NT, GH, NB]), sb("kq", [GR, 2]), sb("sel", [GR, NT, 2], BF16)
        keep, own = sb("keep", [P, GH, NT, NB]), sb("own", [P, GH, NT, NB])
        pr, pt = sb("pr", [P, 2, GH, NT, S]), sb("pt", [P, 2, NT, S])
        prod = pt[:, 0]
        hT = pr[:, 0, 0, 0:DC]
        OT = pr[:, 1, 1, 0:DC]
        V, O = (qk[:, n].rearrange("p a (t d) -> p (a t) d", d=D) for n in range(2))
        o1, o2 = kd[:, :, 0:GH * AD], kd[:, :, GH * AD:2 * GH * AD]
        heads = lambda c: slice(GH * c, GH * c + GH)

        with nc.Block() as block:
            @block.vector
            def _(dve):
                link = Chain(dve, sm["ga_chain"])
                dve.memset(kd[:, :, :], 0.0).then_inc(sm["ga_zero"], 1)
                dve.memset(oT[:, :], 0.0).then_inc(sm["ga_zero"], 1)
                dve.wait_ge(sm["ga_hT"], 1)
                dve.tensor_reduce(hm[:, :, :], hT[:, :, :].rearrange("p c (n k) -> p c n k", k=64), AX.X,
                                  ALU.add).then_inc(sm["ga_sum"], 1)
                dve.wait_ge(sm["ga_zero"], 2)
                dve.wait_ge(sm["ga_qm"], 2)
                dve.tensor_scalar(qm[:, :, :], PS[:, 0, 0:HC * NB].rearrange("p (c n) -> p c n", c=HC), 1 / 64, None,
                                  ALU.mult).then_inc(sm["ga_qmcp"], 1)
                for g in range(HC):
                    ins = dve.tensor_scalar(kd[32 * g:32 * g + 32, :, 32 * g + AD:32 * g + AD + NB],
                                            PS[32 * g:32 * g + 32, 1, 0:HC * NB].rearrange("p (c n) -> p c n", c=HC),
                                            1 / 64, None, ALU.mult)
                ins.then_inc(sm["ga_kd"], 1)
                dve.wait_ge(sm["ga_bs"], 1)
                gview = gate[:, :].rearrange("q (h s) -> q h s", s=32)[:, :, AD:AD + NB]
                dve.tensor_scalar(gview, PS[0:NB, 2, :].rearrange("q (h s) -> q h s", s=32)[:, :, AD:AD + NB],
                                  THRESH * 4, NEG, ALU.is_le, ALU.mult).then_inc(sm["ga_gate"], 1)
                dve.wait_ge(sm["ga_gate"], 1)
                dve.tensor_copy(gate_bf[:, :], gate[:, :]).then_inc(sm["ga_gate"], 1)
                link(dve.tensor_tensor(gd[:, :, :], gview, w["eye8"][:, :].unsqueeze(1).to_broadcast([NB, H, NB]),
                                       ALU.mult))
                dve.tensor_reduce(gdiag[:, :], gd[:, :, :], AX.X, ALU.add).then_inc(sm["ga_md"], 1)
                def evacuate(n):
                    for of in range(0, HC, 2):
                        i = HC * n + of
                        dve.wait_ge(sm["ga_sp"], i + 1)
                        dve.tensor_copy(parts[:, n % 2, HC * (n // 2) + of, :], PS[:, i % 4, :]).then_inc(sm["ga_pd"], 1)

                for n in range(2 * HC):
                    if n >= 2:
                        evacuate(n - 2)
                    if n >= 4:
                        dve.wait_ge(sm["ga_prod"], n // 2 - 1)
                    dve.wait_ge(sm["ga_qk"], n + 1)
                    dve.tensor_scalar(qk[:, n % 2, n // 2 % 2, :], PS[:, 4 + n % 2, :], 0.25 if n % 2 == 0 else 1.0, None,
                                      ALU.mult).then_inc(sm["ga_qkcp"], 1)
                evacuate(2 * HC - 2)
                evacuate(2 * HC - 1)
                dve.wait_ge(sm["ga_prod"], HC)
                dve.wait_ge(sm["ga_v"], 1)
                dve.tensor_copy(V[:, :, :], PS[:, 6:8, :].rearrange("p a (t d) -> p (a t) d", d=D)).then_inc(sm["ga_vcp"], 1)
                dve.wait_ge(sm["ga_mdcp"], 1)
                md = PS[:, 3, 0:NT * H].rearrange("p (t h) -> p t h", t=NT)
                dve.tensor_scalar(masked[:, :, :], md, -1e29, None, ALU.is_lt)
                ins = dve.tensor_scalar(open_[:, :, :], md, -1e29, None, ALU.is_ge)
                link(ins)
                dve.wait_ge(sm["ga_sd"], 1)
                link(dve.tensor_copy(sd[:, :, :], PS[:, 0, 0:NT * H].rearrange("p (t h) -> p t h", t=NT)))
                dve.scalar_tensor_tensor(out=bmax[:, :, :, NB], in0=open_[:, :, :], scalar=NEG, in1=sd[:, :, :],
                                         op0=ALU.mult, op1=ALU.add).then_inc(sm["ga_sde"], 1)
                dve.wait_ge(sm["ga_sde"], 1)

                def maxima(c, k):
                    t, h, n = k, GH * c, NT * c + k
                    dve.wait_ge(sm["ga_S"], n + 1)
                    bank = 2 * (n % 2)
                    link(dve.tensor_reduce(bmax[:, t, h:h + 2, 0:NB],
                                           PS[:, bank:bank + 2, :].rearrange("p a (n k) -> p a n k", k=64), AX.X, ALU.max))
                    dve.tensor_reduce(nm[:, t, h:h + 2], bmax[:, t, h:h + 2, :], AX.X, ALU.max,
                                      negate=True).then_inc(sm["ga_neg"], 1)

                def shifted(c):
                    hs = heads(c)
                    dve.wait_ge(sm["ga_neg"], NT * (c + 1))
                    dve.tensor_tensor(edf[:, :, hs], sd[:, :, hs], nm[:, :, hs], ALU.add)
                    dve.tensor_tensor(aa[:, :, :, :], bmax[:, :, hs, 0:NB],
                                      nm[:, :, hs].unsqueeze(3).to_broadcast([P, NT, GH, NB]), ALU.add)\
                       .then_inc(sm["ga_g1"], 1)

                def block_probabilities(c):
                    hs = heads(c)
                    dve.wait_ge(sm["ga_g2"], c + 1)
                    dve.wait_ge(sm["ga_exp"], NT * (c + 1))
                    link(dve.tensor_tensor(tmp[:, :, hs], edf[:, :, hs], masked[:, :, hs], ALU.mult))
                    link(dve.tensor_tensor(tmp[:, :, hs], tmp[:, :, hs], rs[:, :, hs], ALU.add))
                    link(dve.reciprocal(rden[:, :, hs], tmp[:, :, hs]))
                    dve.tensor_tensor(aa[:, :, :, :], aa[:, :, :, :],
                                      rden[:, :, hs].unsqueeze(3).to_broadcast([P, NT, GH, NB]), ALU.mult)\
                       .then_inc(sm["ga_aa"], 1)

                def block_choice(c):
                    dve.wait_ge(sm["ga_aT"], c + 1)
                    link(dve.tensor_reduce(kq[:, :], PS[0:GR, 7, 0:P].rearrange("p (n k) -> p n k", k=64), AX.X, ALU.max))
                    dve.scalar_tensor_tensor(out=sel[:, :, :], in0=kq[:, :].unsqueeze(1).to_broadcast([GR, NT, 2]),
                                             scalar=THRESH,
                                             in1=w["tile_of"][:, :].unsqueeze(2).to_broadcast([GR, NT, 2]),
                                             op0=ALU.is_gt, op1=ALU.mult).then_inc(sm["ga_D"], 1)

                def keep_factors(c):
                    dve.wait_ge(sm["ga_keep"], c + 1)
                    dve.tensor_copy(keep[:, :, :, :].rearrange("p h t n -> p (h t n)"), PS[:, 7, P:P + GR])\
                       .then_inc(sm["ga_kcp"], 1)
                    dve.wait_ge(sm["ga_kcp"], c + 1)

                def own_keys(c):
                    hs = heads(c)
                    link(dve.tensor_tensor(own[:, :, :, :], keep[:, :, :, :],
                                           w["own_block"][:, :, :].unsqueeze(1).to_broadcast([P, GH, NT, NB]), ALU.mult))
                    link(dve.tensor_reduce(kdg[:, :, :].rearrange("p t h -> p h t"), own[:, :, :, :], AX.X, ALU.add))
                    link(dve.tensor_tensor(tmp[:, :, hs], kdg[:, :, :], open_[:, :, hs], ALU.mult))
                    link(dve.tensor_scalar(tmp[:, :, hs], tmp[:, :, hs], -1.0, 1.0, ALU.mult, ALU.add))
                    link(dve.tensor_tensor(cd[:, :, hs], edf[:, :, hs], rden[:, :, hs], ALU.mult))
                    dve.tensor_tensor(cd[:, :, hs], cd[:, :, hs], tmp[:, :, hs], ALU.mult).then_inc(sm["ga_cd"], 1)

                def move(c, i):
                    h, kt = divmod(i, NT)
                    n = GH * NT * c + i
                    dve.wait_ge(sm["ga_T"], n + 1)
                    if n >= 8:
                        dve.wait_ge(sm["ga_av"], n // NT - 1)
                    dve.tensor_tensor(pt[:, h % 2, kt, :].rearrange("p (n k) -> p n k", k=64),
                                      PS[:, 4 + i % 2, :].rearrange("p (n k) -> p n k", k=64),
                                      keep[:, h, kt, :].unsqueeze(2).to_broadcast([P, NB, 64]), ALU.mult)\
                       .then_inc(sm["ga_ev"], 1)

                def finish(c):
                    hs = heads(c)
                    dve.wait_ge(sm["ga_back"], c + 1)
                    link(dve.tensor_tensor(o1[:, :, :].rearrange("p t (h d) -> p t h d", d=AD),
                                           PS[:, 6, 0:NT * 64].rearrange("p (t h d) -> p t h d", t=NT, d=32)[:, :, :, 0:AD],
                                           rden[:, :, hs].unsqueeze(3).to_broadcast([P, NT, GH, AD]), ALU.mult))
                    dve.wait_ge(sm["ga_cdv"], c + 1)
                    dve.tensor_tensor(O[:, :, GH * AD * c:GH * AD * (c + 1)], o1[:, :, :], o2[:, :, :],
                                      ALU.add).then_inc(sm["ga_Oev"], 1)

                for k in range(NT):
                    maxima(0, k)
                for c in range(NG):
                    more = c + 1 < NG
                    shifted(c)
                    if more:
                        maxima(c + 1, 0)
                    block_probabilities(c)
                    if more:
                        maxima(c + 1, 1)
                    block_choice(c)
                    if more:
                        maxima(c + 1, 2)
                    keep_factors(c)
                    for i in range(GH * NT):
                        if more and i == 1:
                            maxima(c + 1, 3)
                        move(c, i)
                        if c and i == 3:
                            finish(c - 1)
                        if i == 5:
                            own_keys(c)
                finish(NG - 1)
                for c in range(DC):
                    dve.wait_ge(sm["ga_OT"], c + 1)
                    dve.tensor_copy(OT[:, c, :], PS[:, 4 + c, :]).then_inc(sm["ga_OTcp"], 1)
                for k in range(2):
                    dve.wait_ge(sm["ga_out"], k + 1)
                    xv = X[:, bass.ds(b * NT + 2 * k, 2), :]
                    dve.tensor_tensor(xv, xv, PS[:, k, :].rearrange("p (t d) -> p t d", d=D), ALU.add)\
                       .then_inc(sm["ga_x"], 1)

            @block.gpsimd
            def _(pool):
                for n in range(2 * HC):
                    pool.wait_ge(sm["ga_hi"], n + 1)
                    if n >= 2:
                        pool.wait_ge(sm["ga_sp"], HC * (n - 1))
                    pool.tensor_tensor(lo[:, n % 2, :], qk[:, n % 2, n // 2 % 2, :], hi[:, n % 2, :].bitcast(F32),
                                       ALU.subtract).then_inc(sm["ga_lo"], 1)
                    if n % 2:
                        pool.tensor_tensor(prod[:, n // 2, :], qk[:, 0, n // 2 % 2, :], qk[:, 1, n // 2 % 2, :],
                                           ALU.mult).then_inc(sm["ga_prod"], 1)
                for c in range(NG):
                    pool.wait_ge(sm["ga_cd"], c + 1)
                    if c:
                        pool.wait_ge(sm["ga_Oev"], c)
                    if c == 0:
                        pool.wait_ge(sm["ga_vcp"], 1)
                    pool.tensor_tensor(o2[:, :, :].rearrange("p t (h d) -> p t h d", d=AD),
                                       V[:, :, GH * AD * c:GH * AD * (c + 1)].rearrange("p t (h d) -> p t h d", d=AD),
                                       cd[:, :, heads(c)].unsqueeze(3).to_broadcast([P, NT, GH, AD]), ALU.mult)\
                        .then_inc(sm["ga_cdv"], 1)

            @block.scalar
            def _(act):
                act.activation(hT[:, :, :], env["hTs"][:, bass.ds(b * DC, DC), :], ACT.Copy).then_inc(sm["ga_hT"], 1)

                def evacuate(n):
                    for of in range(1, HC, 2):
                        i = HC * n + of
                        act.wait_ge(sm["ga_sp"], i + 1)
                        act.activation(parts[:, n % 2, HC * (n // 2) + of, :], PS[:, i % 4, :],
                                       ACT.Copy).then_inc(sm["ga_pa"], 1)

                for n in range(2 * HC):
                    act.wait_ge(sm["ga_qkcp"], n + 1)
                    if n >= 2:
                        act.wait_ge(sm["ga_sp"], HC * (n - 1))
                        act.wait_ge(sm["ga_lo"], n - 1)
                    act.activation(hi[:, n % 2, :], qk[:, n % 2, n // 2 % 2, :], ACT.Copy).then_inc(sm["ga_hi"], 1)
                    if n:
                        evacuate(n - 1)
                evacuate(2 * HC - 1)

                def exponentials(c, k):
                    n = NT * c + k
                    act.wait_ge(sm["ga_neg"], n + 1)
                    if c >= 2 and k == 0:
                        act.wait_ge(sm["ga_T"], GH * NT * (c - 1))
                    for e in range(GH):
                        h = GH * c + e
                        ins = act.activation(pr[:, c % 2, e, k, :], PS[:, 2 * (n % 2) + e, :], ACT.Exp,
                                             bias=nm[:, k, h:h + 1], accum_out=rs[:, k, h:h + 1])
                    ins.then_inc(sm["ga_exp"], 1)

                def outputs(c, h):
                    act.wait_ge(sm["ga_av"], GH * c + h + 1)
                    if c:
                        act.wait_ge(sm["ga_back"], c)
                    part = slice(32 * h, 32 * h + AD)
                    act.activation(oT[part, :], PS[part, 6, :], ACT.Copy).then_inc(sm["ga_oT"], 1)

                for k in range(NT):
                    exponentials(0, k)
                for c in range(NG):
                    hs = heads(c)
                    act.wait_ge(sm["ga_g1"], c + 1)
                    act.activation(edf[:, :, hs], edf[:, :, hs], ACT.Exp)
                    act.activation(aa[:, :, :, :], aa[:, :, :, :], ACT.Exp).then_inc(sm["ga_g2"], 1)
                    for k in range(NT):
                        if c + 1 < NG:
                            exponentials(c + 1, k)
                        if c and 1 <= k <= GH:
                            outputs(c - 1, k - 1)
                for h in range(GH):
                    outputs(NG - 1, h)

            @block.tensor
            def _(pe):
                pe.wait_ge(sm["ga_hT"], 1)
                pe.wait_ge(sm["ga_sum"], 1)
                for n, name in ((0, "wq"), (1, "wk")):
                    for ch in range(HC):
                        for c in range(DC):
                            ins = pe.matmul(PS[:, n, ch * NB:ch * NB + NB], w[name][:, c, ch * P:ch * P + P], hm[:, c, :],
                                            start=(c == 0), stop=(c == DC - 1))
                    ins.then_inc(sm["ga_qm"], 1)
                pe.wait_ge(sm["ga_qmcp"], 1)
                pe.wait_ge(sm["ga_kd"], 1)
                for ch in range(HC):
                    ins = pe.matmul(PS[0:NB, 2, ch * P:ch * P + P], qm[:, ch, :], kd[:, ch, :], start=True, stop=True)
                ins.then_inc(sm["ga_bs"], 1)
                for t in range(NT):
                    for c in range(DC):
                        ins = pe.matmul(PS[:, 6 + t // 2, t % 2 * D:t % 2 * D + D], hT[:, c, t * P:t * P + P],
                                        w["wv"][:, c, :], start=(c == 0), stop=(c == DC - 1))
                ins.then_inc(sm["ga_v"], 1)
                pe.wait_ge(sm["ga_gate"], 2)

                def spread(n):
                    pe.wait_ge(sm["ga_hi"], n + 1)
                    pe.wait_ge(sm["ga_lo"], n + 1)
                    for of in range(HC):
                        i = HC * n + of
                        if i == 0:
                            pe.wait_ge(sm["ga_kd"], 1)
                            pe.wait_ge(sm["ga_qmcp"], 1)
                        if i >= 4:
                            pe.wait_ge(sm["ga_pa" if i % 2 else "ga_pd"], i // 2 - 1)
                        pe.matmul(PS[:, i % 4, :], w["spread"][:, 2 * (n % 2), of, :], hi[:, n % 2, :], start=True,
                                  stop=False)
                        pe.matmul(PS[:, i % 4, :], w["spread"][:, 2 * (n % 2) + 1, of, :], lo[:, n % 2, :], start=False,
                                  stop=True).then_inc(sm["ga_sp"], 1)

                for n in range(2 * HC):
                    if n >= 2:
                        pe.wait_ge(sm["ga_qkcp"], n - 1)
                    name, ch = ("wq", "wk")[n % 2], n // 2
                    for c in range(DC):
                        pe.matmul(PS[:, 4 + n % 2, :], w[name][:, c, ch * P:ch * P + P], hT[:, c, :],
                                  start=(c == 0), stop=False)
                    rows = gate_bf[:, ch * P:ch * P + P] if n % 2 == 0 else w["key_rows_bf"][:, :]
                    pe.matmul(PS[:, 4 + n % 2, :], rows, w["blocks_bf"][:, :], start=False,
                              stop=True).then_inc(sm["ga_qk"], 1)
                    if n:
                        spread(n - 1)
                spread(2 * HC - 1)
                pe.wait_ge(sm["ga_pd"], H)
                pe.wait_ge(sm["ga_pa"], H)
                pe.wait_ge(sm["ga_md"], 1)
                for t in range(NT):
                    ins = pe.matmul(PS[:, 3, t * H:t * H + H], w["blocks"][:, t * P:t * P + P], gdiag[:, :],
                                    start=True, stop=True)
                ins.then_inc(sm["ga_mdcp"], 1)
                pe.wait_ge(sm["ga_prod"], HC)
                for t in range(NT):
                    for ch in range(HC):
                        ins = pe.matmul(PS[:, 0, t * H:t * H + H], prod[:, ch, t * P:t * P + P], w["head4"][:, ch, :],
                                        start=(ch == 0), stop=(ch == HC - 1))
                ins.then_inc(sm["ga_sd"], 1)
                pe.wait_ge(sm["ga_sde"], 1)

                def scores(c, k):
                    n = NT * c + k
                    if n >= 2:
                        pe.wait_ge(sm["ga_exp"], n - 1)
                    for e in range(GH):
                        h = GH * c + e
                        ins = pe.matmul(PS[:, 2 * (n % 2) + e, :], parts[:, 0, h, k * P:k * P + P], parts[:, 1, h, :],
                                        start=True, stop=True)
                    ins.then_inc(sm["ga_S"], 1)

                def turn(c, i):
                    h, kt = divmod(i, NT)
                    n = GH * NT * c + i
                    if n >= 2:
                        pe.wait_ge(sm["ga_ev"], n - 1)
                    for t in range(NT):
                        ins = pe.transpose(PS[:, 4 + i % 2, t * P:t * P + P], pr[:, c % 2, h, t, kt * P:kt * P + P], ident)
                    ins.then_inc(sm["ga_T"], 1)

                def values(c, h):
                    pe.wait_ge(sm["ga_ev"], GH * NT * c + NT * (h + 1))
                    if h == 0 and c == 0:
                        pe.wait_ge(sm["ga_vcp"], 1)
                    if h == 0 and c:
                        pe.wait_ge(sm["ga_Oev"], c)
                    col = (GH * c + h) * AD
                    for kt in range(NT):
                        ins = pe.matmul(PS[32 * h:32 * h + AD, 6, :], V[:, kt, col:col + AD], pt[:, h, kt, :],
                                        start=(kt == 0), stop=(kt == NT - 1), tile_position=(0, 32 * h))
                    ins.then_inc(sm["ga_av"], 1)

                def back(c):
                    pe.wait_ge(sm["ga_oT"], GH * (c + 1))
                    for t in range(NT):
                        ins = pe.transpose(PS[:, 6, t * 64:t * 64 + OR], oT[:, t * P:t * P + P], ident[0:OR, 0:OR])
                    ins.then_inc(sm["ga_back"], 1)

                for k in range(NT):
                    scores(0, k)
                for c in range(NG):
                    more = c + 1 < NG
                    if more:
                        scores(c + 1, 0)
                        scores(c + 1, 1)
                    if c:
                        values(c - 1, 0)
                    pe.wait_ge(sm["ga_aa"], c + 1)
                    pe.transpose(PS[0:GR, 7, 0:P], aa[:, :, :, :].rearrange("p t h n -> p (t h n)"), ident)\
                      .then_inc(sm["ga_aT"], 1)
                    if more:
                        scores(c + 1, 2)
                    pe.wait_ge(sm["ga_D"], c + 1)
                    for n in range(GH * NT):
                        ins = pe.matmul(PS[:, 7, P + n * NB:P + n * NB + NB], w["pick"][:, n, :],
                                        sel[:, :, :].rearrange("p t q -> p (t q)"), start=True, stop=True)
                    ins.then_inc(sm["ga_keep"], 1)
                    if c:
                        values(c - 1, 1)
                    for i in range(GH * NT):
                        if more and i == 1:
                            scores(c + 1, 3)
                        turn(c, i)
                        if c and i == 2:
                            back(c - 1)
                for h in range(GH):
                    values(NG - 1, h)
                back(NG - 1)
                pe.wait_ge(sm["ga_Oev"], NG)
                for c in range(DC):
                    for t in range(NT):
                        ins = pe.transpose(PS[:, 4 + c, t * P:t * P + P], O[:, t, c * P:c * P + P], ident)
                    ins.then_inc(sm["ga_OT"], 1)
                pe.wait_ge(sm["ga_OTcp"], DC)
                for t in range(NT):
                    for c in range(DC):
                        ins = pe.matmul(PS[:, t // 2, t % 2 * D:t % 2 * D + D], OT[:, c, t * P:t * P + P],
                                        w["wo"][:, c, :], start=(c == 0), stop=(c == DC - 1))
                    if t % 2:
                        ins.then_inc(sm["ga_out"], 1)
        nc.all_engine_barrier(sems_to_clear=sm.all)


NE = 8
EW = 128
NX = NE + 2
G = 64


def experts_weights(nc, env, ctx, layer):
    a, pre = env["dram"], f"L{layer}_cond2_"
    sb = lambda n, s, d=F32: ctx.enter_context(nc.sbuf_tensor(f"ex{layer}_" + n, s, d))
    w = {"gate": sb("gate", [P, DC, NX, EW]), "up": sb("up", [P, DC, NX, EW]), "down": sb("down", [P, NX, D]),
         "wt": sb("wt", [P, DC, NE]), "wg": sb("wg", [G, NE]), "cond": sb("cond", [G, B]),
         "first": sb("first", [P, NE]), "row_of": sb("row_of", [NE, NE, P])}
    with ExitStack() as inner:
        sm = Sems(inner, nc, "ew_in")
        with nc.Block() as block:
            @block.sync
            def _(sp):
                def load(dst, src):
                    sp.dma_start(dst, src).then_inc(sm["ew_in"], 16)

                for c in range(DC):
                    rows = slice(c * P, c * P + P)
                    for n in ("gate", "up"):
                        load(w[n][:, c, 0:NE, :], a[pre + "w_" + n][:, rows, :].rearrange("e p m -> p e m"))
                        load(w[n][:, c, NE:NX, :], a[pre + "sw_" + n][rows, :].rearrange("p (e m) -> p e m", m=EW))
                load(w["down"][:, 0:NE, :], a[pre + "w_down"].rearrange("e m h -> m e h"))
                load(w["down"][:, NE:NX, :], a[pre + "sw_down"].rearrange("(e m) h -> m e h", m=EW))
                load(w["wt"][:, :, :], a[pre + "wt"].rearrange("(c p) e -> p c e", p=P))
                load(w["wg"][:, :], a[pre + "wg"])
                load(w["cond"][:, :], a["cond_columns"])
                load(w["first"][:, :], a["c_first"])
                load(w["row_of"][:, :, :], a["c_row_of"])
                sp.wait_ge(sm["ew_in"], 16 * 15)
        nc.all_engine_barrier(sems_to_clear=sm.all)
    return w


EXPERT_SEMS = ("ex_xb ex_chain ex_cond ex_xT ex_xTd ex_xTa ex_lg ex_ready ex_exp ex_comb ex_cT ex_cTcp ex_gate ex_up ex_spread "
               "ex_gcp ex_lk ex_hu ex_h ex_down ex_y ex_rows ex_rowscp")


def experts(nc, env, sm, w, b, yT, layer):
    X, PS, ident = env["X"], env["PS"], env["ident"]
    with ExitStack() as ctx:
        sb = lambda n, s, d=F32: ctx.enter_context(nc.sbuf_tensor(f"eb{layer}_" + n, s, d))
        xb, xT, cb = sb("xb", [P, NT, D]), sb("xT", [P, DC, S]), sb("cb", [G, P])
        lg, sc, pri, s1, s2, sc2 = (sb(n, [P, NT, NE]) for n in ("lg", "sc", "pri", "s1", "s2", "sc2"))
        mx, su, m1, m2, pm = (sb(n, [P, NT]) for n in ("mx", "su", "m1", "m2", "pm"))
        cT = sb("cT", [NE, S])
        gs, lk, hu, hx = (sb(n, [P, 2, S]) for n in ("gs", "lk", "hu", "hx"))
        wide = lambda v: v[:, :].unsqueeze(2).to_broadcast([P, NT, NE])
        with nc.Block() as block:
            @block.vector
            def _(dve):
                link = Chain(dve, sm["ex_chain"])
                dve.tensor_copy(cb[:, :], w["cond"][:, bass.ds(b, 1)].to_broadcast([G, P])).then_inc(sm["ex_cond"], 1)
                dve.wait_ge(sm["ex_xT"], 1)
                dve.tensor_copy(xT[:, 0, :], PS[:, 0, :]).then_inc(sm["ex_xTd"], 1)
                dve.wait_ge(sm["ex_lg"], 1)
                link(dve.tensor_scalar(lg[:, :, :], PS[:, 4, 0:NT * NE].rearrange("p (t e) -> p t e", t=NT), 0.5, None,
                                       ALU.mult))
                link(dve.tensor_reduce(mx[:, :], lg[:, :, :], AX.X, ALU.max))
                dve.tensor_tensor(lg[:, :, :], lg[:, :, :], wide(mx), ALU.subtract).then_inc(sm["ex_ready"], 1)

                def route():
                    dve.wait_ge(sm["ex_exp"], 1)
                    link(dve.tensor_reduce(su[:, :], lg[:, :, :], AX.X, ALU.add))
                    link(dve.reciprocal(su[:, :], su[:, :]))
                    link(dve.tensor_tensor(sc[:, :, :], lg[:, :, :], wide(su), ALU.mult))
                    first = w["first"][:, :].unsqueeze(1).to_broadcast([P, NT, NE])

                    def pick(scores, top, chosen):
                        link(dve.tensor_reduce(top[:, :], scores[:, :, :], AX.X, ALU.max))
                        link(dve.tensor_tensor(pri[:, :, :], scores[:, :, :], wide(top), ALU.is_equal))
                        link(dve.tensor_tensor(pri[:, :, :], pri[:, :, :], first, ALU.mult))
                        link(dve.tensor_reduce(pm[:, :], pri[:, :, :], AX.X, ALU.max))
                        link(dve.tensor_tensor(chosen[:, :, :], pri[:, :, :], wide(pm), ALU.is_equal))

                    pick(sc, m1, s1)
                    link(dve.tensor_scalar(sc2[:, :, :], s1[:, :, :], -1.0, 1.0, ALU.mult, ALU.add))
                    link(dve.tensor_tensor(sc2[:, :, :], sc2[:, :, :], sc[:, :, :], ALU.mult))
                    link(dve.tensor_tensor(sc2[:, :, :], sc2[:, :, :], s1[:, :, :], ALU.subtract))
                    pick(sc2, m2, s2)
                    link(dve.scalar_tensor_tensor(out=m1[:, :], in0=m1[:, :], scalar=1e-20, in1=m2[:, :], op0=ALU.add,
                                                  op1=ALU.add))
                    link(dve.reciprocal(m1[:, :], m1[:, :]))
                    link(dve.tensor_tensor(s1[:, :, :], s1[:, :, :], s2[:, :, :], ALU.add))
                    link(dve.tensor_tensor(s1[:, :, :], s1[:, :, :], sc[:, :, :], ALU.mult))
                    dve.tensor_tensor(s1[:, :, :], s1[:, :, :], wide(m1), ALU.mult).then_inc(sm["ex_comb"], 1)
                    dve.wait_ge(sm["ex_cT"], 1)
                    dve.tensor_copy(cT[:, :], PS[0:NE, 7, :]).then_inc(sm["ex_cTcp"], 1)

                for e in range(NX):
                    if e == 1:
                        route()
                    dve.wait_ge(sm["ex_gcp"], e + 1)
                    dve.scalar_tensor_tensor(out=lk[:, e % 2, :], in0=gs[:, e % 2, :], scalar=0.01, in1=gs[:, e % 2, :],
                                             op0=ALU.mult, op1=ALU.max).then_inc(sm["ex_lk"], 1)
                    dve.wait_ge(sm["ex_lk"], e + 1)
                    dve.wait_ge(sm["ex_up"], e + 1)
                    if e >= NE and e >= 2:
                        dve.wait_ge(sm["ex_down"], e - 1)
                    dst = hu if e < NE else hx
                    ins = dve.tensor_tensor(dst[:, e % 2, :], lk[:, e % 2, :], PS[:, 3 + 3 * (e % 2), :], ALU.mult)
                    ins.then_inc(sm["ex_hu"], 1)
                    if e >= 1 and e - 1 < NE:
                        k = e - 1
                        dve.wait_ge(sm["ex_hu"], e)
                        dve.wait_ge(sm["ex_spread"], k + 1)
                        if k >= 2:
                            dve.wait_ge(sm["ex_down"], k - 1)
                        dve.tensor_tensor(hx[:, k % 2, :], hu[:, k % 2, :], PS[:, 4 + 3 * (k % 2), :],
                                          ALU.mult).then_inc(sm["ex_h"], 1)
                for c in range(DC):
                    dve.wait_ge(sm["ex_down"], NX)
                    dve.tensor_copy(yT[:, c, :], PS[:, c, :]).then_inc(sm["ex_y"], 1)

            @block.scalar
            def _(act):
                act.activation(xb[:, :, :], X[:, bass.ds(b * NT, NT), :], ACT.Copy).then_inc(sm["ex_xb"], 1)
                act.wait_ge(sm["ex_xT"], 2)
                act.activation(xT[:, 1, :], PS[:, 1, :], ACT.Copy).then_inc(sm["ex_xTa"], 1)
                for e in range(NX):
                    if e == 1:
                        act.wait_ge(sm["ex_ready"], 1)
                        act.activation(lg[:, :, :], lg[:, :, :], ACT.Exp).then_inc(sm["ex_exp"], 1)
                    act.wait_ge(sm["ex_gate"], e + 1)
                    if e >= 2:
                        act.wait_ge(sm["ex_lk"], e - 1)
                    act.activation(gs[:, e % 2, :], PS[:, 2 + 3 * (e % 2), :], ACT.Copy).then_inc(sm["ex_gcp"], 1)

            @block.tensor
            def _(pe):
                pe.wait_ge(sm["ex_xb"], 1)
                for c in range(DC):
                    for t in range(NT):
                        ins = pe.transpose(PS[:, c, t * P:t * P + P], xb[:, t, c * P:c * P + P], ident)
                    ins.then_inc(sm["ex_xT"], 1)
                pe.wait_ge(sm["ex_xTd"], 1)
                pe.wait_ge(sm["ex_xTa"], 1)
                pe.wait_ge(sm["ex_cond"], 1)
                for t in range(NT):
                    o = PS[:, 4, t * NE:t * NE + NE]
                    for c in range(DC):
                        pe.matmul(o, xT[:, c, t * P:t * P + P], w["wt"][:, c, :], start=(c == 0), stop=False)
                    ins = pe.matmul(o, cb[:, :], w["wg"][:, :], start=False, stop=True)
                ins.then_inc(sm["ex_lg"], 1)

                def spread(e):
                    if e == 0:
                        pe.wait_ge(sm["ex_comb"], 1)
                        for t in range(NT):
                            ins = pe.transpose(PS[0:NE, 7, t * P:t * P + P], s1[:, t, :], ident)
                        ins.then_inc(sm["ex_cT"], 1)
                        pe.wait_ge(sm["ex_cTcp"], 1)
                    if e >= 2:
                        pe.wait_ge(sm["ex_h"], e - 1)
                    pe.matmul(PS[:, 4 + 3 * (e % 2), :], w["row_of"][:, e, :], cT[:, :], start=True,
                              stop=True).then_inc(sm["ex_spread"], 1)

                def down(e):
                    if e < NE:
                        pe.wait_ge(sm["ex_h"], e + 1)
                    else:
                        pe.wait_ge(sm["ex_hu"], e + 1)
                    for c in range(DC):
                        ins = pe.matmul(PS[:, c, :], w["down"][:, e, c * P:c * P + P], hx[:, e % 2, :], start=(e == 0),
                                        stop=(e == NX - 1))
                    ins.then_inc(sm["ex_down"], 1)

                for e in range(NX + 2):
                    if e < NX:
                        for n, name, sem in ((2, "gate", "ex_gate"), (3, "up", "ex_up")):
                            if e >= 2:
                                pe.wait_ge(sm["ex_gcp" if n == 2 else "ex_hu"], e - 1)
                            for c in range(DC):
                                ins = pe.matmul(PS[:, n + 3 * (e % 2), :], w[name][:, c, e, :], xT[:, c, :],
                                                start=(c == 0), stop=(c == DC - 1))
                            ins.then_inc(sm[sem], 1)
                    if 1 <= e <= NE:
                        spread(e - 1)
                    if e >= 2:
                        down(e - 2)
        nc.all_engine_barrier(sems_to_clear=sm.all)


DF = 1024
FC = DF // P


def ffn_weights(nc, env, ctx):
    a = env["dram"]
    sb = lambda n, s, d=F32: ctx.enter_context(nc.sbuf_tensor("ff_" + n, s, d))
    w = {"w1": sb("w1", [P, DC, DF]), "w2": sb("w2", [P, DC, DF]), "h1": sb("h1", [P, FC, DF]), "h2": sb("h2", [P, FC, DF]),
         "w3": sb("w3", [P, FC, D]), "s3": sb("s3", [P, D])}
    for n in ("w1", "w2", "h1", "h2"):
        w[n + "_s"] = sb(n + "_s", [P, FC])
    w["loaded"] = sm = env["loads"]
    with nc.Block() as block:
        @block.sync
        def _(sp):
            for n in ("w1", "w2", "h1", "h2", "w3"):
                sp.dma_start(w[n][:, :, :], a[f"L0_ffn_{n}_w"].rearrange("(c p) n -> p c n", p=P))\
                  .then_inc(sm["fw_in"], 16)
            for n in ("w1", "w2", "h1", "h2"):
                sp.dma_start(w[n + "_s"][:, :], a[f"L0_ffn_{n}_s"]).then_inc(sm["fw_in"], 16)
            sp.dma_start(w["s3"][:, :], a["L0_ffn_w3_s"].unsqueeze(0).to_broadcast([P, D])).then_inc(sm["fw_in"], 16)
    return w


FFN_SEMS = "ff_a ff_b ff_silu ff_g1 ff_m1 ff_g2 ff_m2 ff_g3 ff_o ff_sc ff_x"


def ffn(nc, env, sm, w, b, yT):
    X, PS = env["X"], env["PS"]
    with ExitStack() as ctx:
        sb = lambda n, s, d=F32: ctx.enter_context(nc.sbuf_tensor("fb_" + n, s, d))
        g1, g2, sa, ot = sb("g1", [P, FC, S]), sb("g2", [P, FC, S]), sb("sa", [P, 2, S]), sb("ot", [P, 2, D])
        with nc.Block() as block:
            @block.vector
            def _(dve):
                dve.wait_ge(w["loaded"]["fw_in"], 16 * 10)
                for m in range(FC):
                    dve.wait_ge(sm["ff_silu"], m + 1)
                    dve.wait_ge(sm["ff_b"], m + 1)
                    dve.scalar_tensor_tensor(out=g1[:, m, :], in0=PS[:, 2 + m % 2, :], scalar=w["w2_s"][:, m:m + 1],
                                             in1=sa[:, m % 2, :], op0=ALU.mult, op1=ALU.mult).then_inc(sm["ff_g1"], 1)
                for k in range(2):
                    dve.wait_ge(sm["ff_o"], k + 1)
                    dve.tensor_tensor(ot[:, :, :], PS[:, 6 + k, :].rearrange("p (t d) -> p t d", d=D),
                                      w["s3"][:, :].unsqueeze(1).to_broadcast([P, 2, D]), ALU.mult).then_inc(sm["ff_sc"], 1)
                    dve.wait_ge(sm["ff_sc"], k + 1)
                    xv = X[:, bass.ds(b * NT + 2 * k, 2), :]
                    dve.tensor_tensor(xv, xv, ot[:, :, :], ALU.add).then_inc(sm["ff_x"], 1)
                    dve.wait_ge(sm["ff_x"], k + 1)

            @block.scalar
            def _(act):
                act.wait_ge(w["loaded"]["fw_in"], 16 * 10)
                for m in range(FC):
                    act.wait_ge(sm["ff_a"], m + 1)
                    if m >= 2:
                        act.wait_ge(sm["ff_g1"], m - 1)
                    act.activation(sa[:, m % 2, :], PS[:, m % 2, :], ACT.Silu, scale=w["w1_s"][:, m:m + 1])\
                       .then_inc(sm["ff_silu"], 1)
                for layer, dst in ((1, g2), (2, g1)):
                    if layer == 2:
                        act.wait_ge(sm["ff_m1"], FC)
                    for m in range(FC):
                        act.wait_ge(sm[f"ff_m{layer}"], m + 1)
                        act.activation(dst[:, m, :], PS[:, 4 + m % 2, :], ACT.Gelu,
                                       scale=w[f"h{layer}_s"][:, m:m + 1]).then_inc(sm[f"ff_g{layer + 1}"], 1)

            @block.tensor
            def _(pe):
                pe.wait_ge(w["loaded"]["fw_in"], 16 * 10)
                for m in range(FC):
                    for n, name, free, sem in ((0, "w1", "ff_silu", "ff_a"), (2, "w2", "ff_g1", "ff_b")):
                        if m >= 2:
                            pe.wait_ge(sm[free], m - 1)
                        for c in range(DC):
                            ins = pe.matmul(PS[:, n + m % 2, :], w[name][:, c, m * P:m * P + P], yT[:, c, :],
                                            start=(c == 0), stop=(c == DC - 1))
                        ins.then_inc(sm[sem], 1)
                for layer, src in ((1, g1), (2, g2)):
                    for m in range(FC):
                        if m >= 2:
                            pe.wait_ge(sm[f"ff_g{layer + 1}"], m - 1)
                        elif layer == 2:
                            pe.wait_ge(sm["ff_g2"], FC - 1 + m)
                        for k in range(FC):
                            if m == 0:
                                pe.wait_ge(sm[f"ff_g{layer}"], k + 1)
                            ins = pe.matmul(PS[:, 4 + m % 2, :], w[f"h{layer}"][:, k, m * P:m * P + P], src[:, k, :],
                                            start=(k == 0), stop=(k == FC - 1))
                        ins.then_inc(sm[f"ff_m{layer}"], 1)
                pe.wait_ge(sm["ff_g3"], FC)
                for t in range(NT):
                    for k in range(FC):
                        ins = pe.matmul(PS[:, 6 + t // 2, t % 2 * D:t % 2 * D + D], g1[:, k, t * P:t * P + P],
                                        w["w3"][:, k, :], start=(k == 0), stop=(k == FC - 1))
                    if t % 2:
                        ins.then_inc(sm["ff_o"], 1)
        nc.all_engine_barrier(sems_to_clear=sm.all)


def chunked_attention_weights(nc, env, ctx):
    a = env["dram"]
    sb = lambda n, s, d=F32: ctx.enter_context(nc.sbuf_tensor("cc_" + n, s, d))
    w = {"wq": sb("wq", [P, DC, HC * P]), "wk": sb("wk", [P, DC, HC * P]), "wv": sb("wv", [P, DC, D]),
         "wo": sb("wo", [P, DC, D]), "bq": sb("bq", [P, HC]), "bk": sb("bk", [P, HC]), "bv": sb("bv", [P, D]),
         "bo": sb("bo", [P, D]), "mean_of": sb("mean_of", [P, NT, H * NT]), "head_rows": sb("head_rows", [H * NT, D]),
         "later": sb("later", [P, NT, NT])}
    with ExitStack() as inner:
        raw = {n: inner.enter_context(nc.sbuf_tensor("cc_raw" + n, [P, DC, D], F32)) for n in ("wq", "wk")}
        sm = Sems(inner, nc, "kw_in kw_zero kw_spread")
        with nc.Block() as block:
            @block.sync
            def _(sp):
                for n in ("wq", "wk", "wv", "wo"):
                    dst = raw[n] if n in raw else w[n]
                    sp.dma_start(dst[:, :, :], a["L1_attn_" + n].rearrange("(c p) n -> p c n", p=P))\
                      .then_inc(sm["kw_in"], 16)
                for n in ("bv", "bo"):
                    sp.dma_start(w[n][:, :], a["L1_attn_" + n].unsqueeze(0).to_broadcast([P, D])).then_inc(sm["kw_in"], 16)
                sp.dma_start(w["mean_of"][:, :, :], a["c_mean_of"]).then_inc(sm["kw_in"], 16)
                sp.dma_start(w["head_rows"][:, :], a["c_head_rows"]).then_inc(sm["kw_in"], 16)
                sp.dma_start(w["later"][:, :, :], a["c_later"]).then_inc(sm["kw_in"], 16)
                sp.wait_ge(sm["kw_zero"], 4)
                for n in ("bq", "bk"):
                    for g in range(HC):
                        sp.dma_start(w[n][32 * g:32 * g + AD, :], a["L1_attn_" + n][g]).then_inc(sm["kw_in"], 16)

            @block.vector
            def _(dve):
                for n in raw:
                    dve.memset(w[n][:, :, :], 0.0).then_inc(sm["kw_zero"], 1)
                for n in ("bq", "bk"):
                    dve.memset(w[n][:, :], 0.0).then_inc(sm["kw_zero"], 1)
                dve.wait_ge(sm["kw_zero"], 4)
                dve.wait_ge(sm["kw_in"], 17 * 16)
                for n in raw:
                    for c in range(DC):
                        dve.tensor_copy(w[n][:, c, :].rearrange("p (h d) -> p h d", d=32)[:, :, 0:AD],
                                        raw[n][:, c, :].rearrange("p (h d) -> p h d", d=AD)).then_inc(sm["kw_spread"], 1)
                dve.wait_ge(sm["kw_spread"], 4)
        nc.all_engine_barrier(sems_to_clear=sm.all)
    return w


CHUNKED_SEMS = ("cc_chain cc_qk cc_qkcp cc_v cc_vcp cc_ones cc_km cc_vm cc_vmcp cc_si cc_sub cc_ie cc_ai cc_aiT cc_aiTcp "
                "cc_S cc_sub2 cc_exp cc_T cc_evd cc_eva cc_av cc_Oev cc_OT cc_OTcp cc_out cc_ob cc_x")


def chunked_attention(nc, env, sm, w, b):
    X, PS, ident, hT = env["X"], env["PS"], env["ident"], env["hT"]
    AV = AD + 1
    with ExitStack() as ctx:
        sb = lambda n, s, d=F32: ctx.enter_context(nc.sbuf_tensor("cd_" + n, s, d))
        qk, V = sb("qk", [P, 2, HC, S]), sb("V", [P, NT, H, AV])
        km, kb = sb("km", [P, HC, NT]), sb("kb", [P, HC, HC * NT])
        si, ai = sb("si", [P, NT, H, NT]), sb("ai", [P, NT, H, NT])
        mi, ri = sb("mi", [P, NT, H]), sb("ri", [P, NT, H])
        aiT, vm = sb("aiT", [H * NT, S]), sb("vm", [H * NT, D])
        mx = sb("mx", [P, 2, H])
        sc, pr, pt = sb("sc", [P, 2, H, P]), sb("pr", [P, 2, H, P]), sb("pt", [P, 2, S])
        rden, O, OT, ob = sb("rden", [P, H]), sb("O", [P, NT, D]), sb("OT", [P, DC, S]), sb("ob", [P, 2, D])
        with nc.Block() as block:
            @block.vector
            def _(dve):
                link = Chain(dve, sm["cc_chain"])
                link(dve.memset(kb[:, :, :], 0.0))
                dve.memset(V[:, :, :, AD], 1.0).then_inc(sm["cc_ones"], 1)
                for n in range(2 * HC):
                    dve.wait_ge(sm["cc_qk"], n + 1)
                    bias = w[("bq", "bk")[n % 2]]
                    dve.tensor_scalar(qk[:, n % 2, n // 2, :], PS[:, 4 + n % 2, :], bias[:, n // 2:n // 2 + 1],
                                      0.25 if n % 2 == 0 else 1.0, ALU.add, ALU.mult).then_inc(sm["cc_qkcp"], 1)
                dve.wait_ge(sm["cc_v"], 1)
                for k in range(2):
                    ins = dve.tensor_tensor(V[:, 2 * k:2 * k + 2, :, 0:AD],
                                            PS[:, 6 + k, :].rearrange("p (t h d) -> p t h d", t=2, d=AD),
                                            w["bv"][:, :].rearrange("p (h d) -> p h d", d=AD).unsqueeze(1)
                                            .to_broadcast([P, 2, H, AD]), ALU.add)
                ins.then_inc(sm["cc_vcp"], 1)
                dve.wait_ge(sm["cc_qkcp"], 2 * HC)
                link(dve.tensor_reduce(km[:, :, :], qk[:, 1].rearrange("p c (j k) -> p c j k", k=P), AX.X, ALU.add))
                for g in range(HC):
                    part = slice(32 * g, 32 * g + 32)
                    ins = dve.tensor_scalar(kb[part, :, NT * g:NT * g + NT], km[part, :, :], 1 / P, None, ALU.mult)
                ins.then_inc(sm["cc_km"], 1)
                dve.wait_ge(sm["cc_vm"], 1)
                dve.tensor_tensor(vm[:, :], PS[0:H * NT, 4, 0:D], w["head_rows"][:, :], ALU.mult).then_inc(sm["cc_vmcp"], 1)
                dve.wait_ge(sm["cc_si"], 1)
                link(dve.tensor_tensor(si[:, :, :, :], PS[:, 5, 0:NT * H * NT].rearrange("p (t h j) -> p t h j", t=NT, j=NT),
                                       w["later"][:, :, :].unsqueeze(2).to_broadcast([P, NT, H, NT]), ALU.add))
                link(dve.tensor_reduce(mi[:, :, :], si[:, :, :, :], AX.X, ALU.max))
                dve.tensor_tensor(si[:, :, :, :], si[:, :, :, :], mi[:, :, :].unsqueeze(3).to_broadcast([P, NT, H, NT]),
                                  ALU.subtract).then_inc(sm["cc_sub"], 1)

                s4 = PS[:, 0:4, :].rearrange("p g (c k) -> p (g c) k", k=P)

                def maxima(t):
                    dve.wait_ge(sm["cc_S"], t + 1)
                    link(dve.tensor_reduce(mx[:, t % 2, :], s4, AX.X, ALU.max))

                def shifted(t):
                    if t >= 2:
                        dve.wait_ge(sm["cc_exp"], t - 1)
                    dve.tensor_tensor(sc[:, t % 2], s4, mx[:, t % 2, :].unsqueeze(2).to_broadcast([P, H, P]),
                                      ALU.subtract).then_inc(sm["cc_sub2"], 1)

                maxima(0)
                shifted(0)
                dve.wait_ge(sm["cc_ie"], 1)
                link(dve.tensor_reduce(ri[:, :, :], si[:, :, :, :], AX.X, ALU.add))
                link(dve.reciprocal(ri[:, :, :], ri[:, :, :]))
                dve.tensor_tensor(ai[:, :, :, :], si[:, :, :, :], ri[:, :, :].unsqueeze(3).to_broadcast([P, NT, H, NT]),
                                  ALU.mult).then_inc(sm["cc_ai"], 1)
                dve.wait_ge(sm["cc_aiT"], 1)
                dve.tensor_copy(aiT[:, :], PS[0:H * NT, 4, :]).then_inc(sm["cc_aiTcp"], 1)
                for t in range(NT):
                    for g in (0, 2):
                        dve.wait_ge(sm["cc_T"], HC * t + g + 1)
                        if HC * t + g >= 2:
                            dve.wait_ge(sm["cc_av"], HC * t + g - 1)
                        dve.tensor_copy(pt[:, 0, :], PS[:, 4, :]).then_inc(sm["cc_evd"], 1)
                        if t + 1 < NT:
                            if g == 0:
                                maxima(t + 1)
                            else:
                                shifted(t + 1)
                    dve.wait_ge(sm["cc_av"], HC * (t + 1))
                    inside = PS[:, 6, 0:H * AV].rearrange("p (h d) -> p h d", d=AV)
                    ot = O[:, t, :].rearrange("p (h d) -> p h d", d=AD)
                    link(dve.reciprocal(rden[:, :], inside[:, :, AD]))
                    link(dve.tensor_tensor(ot, inside[:, :, 0:AD], rden[:, :].unsqueeze(2).to_broadcast([P, H, AD]),
                                           ALU.mult))
                    dve.tensor_tensor(O[:, t, :], O[:, t, :], PS[:, 7, 0:D], ALU.add).then_inc(sm["cc_Oev"], 1)
                for c in range(DC):
                    dve.wait_ge(sm["cc_OT"], c + 1)
                    dve.tensor_copy(OT[:, c, :], PS[:, c, :]).then_inc(sm["cc_OTcp"], 1)
                for k in range(2):
                    dve.wait_ge(sm["cc_out"], k + 1)
                    dve.tensor_tensor(ob[:, :, :], PS[:, 2 + k, :].rearrange("p (t d) -> p t d", d=D),
                                      w["bo"][:, :].unsqueeze(1).to_broadcast([P, 2, D]), ALU.add).then_inc(sm["cc_ob"], 1)
                    dve.wait_ge(sm["cc_ob"], k + 1)
                    xv = X[:, bass.ds(b * NT + 2 * k, 2), :]
                    dve.tensor_tensor(xv, xv, ob[:, :, :], ALU.add).then_inc(sm["cc_x"], 1)
                    dve.wait_ge(sm["cc_x"], k + 1)

            @block.scalar
            def _(act):
                act.wait_ge(sm["cc_sub"], 1)
                act.activation(si[:, :, :, :], si[:, :, :, :], ACT.Exp).then_inc(sm["cc_ie"], 1)

                def exponential(t):
                    act.wait_ge(sm["cc_sub2"], t + 1)
                    if t >= 2:
                        act.wait_ge(sm["cc_T"], HC * (t - 1))
                    act.activation(pr[:, t % 2], sc[:, t % 2], ACT.Exp).then_inc(sm["cc_exp"], 1)

                exponential(0)
                for t in range(NT):
                    for g in (1, 3):
                        act.wait_ge(sm["cc_T"], HC * t + g + 1)
                        if HC * t + g >= 2:
                            act.wait_ge(sm["cc_av"], HC * t + g - 1)
                        act.activation(pt[:, 1, :], PS[:, 5, :], ACT.Copy).then_inc(sm["cc_eva"], 1)
                    if t + 1 < NT:
                        exponential(t + 1)

            @block.tensor
            def _(pe):
                for n in range(2 * HC):
                    if n >= 2:
                        pe.wait_ge(sm["cc_qkcp"], n - 1)
                    name, ch = ("wq", "wk")[n % 2], n // 2
                    for c in range(DC):
                        ins = pe.matmul(PS[:, 4 + n % 2, :], w[name][:, c, ch * P:ch * P + P], hT[:, c, :],
                                        start=(c == 0), stop=(c == DC - 1))
                    ins.then_inc(sm["cc_qk"], 1)
                for t in range(NT):
                    for c in range(DC):
                        ins = pe.matmul(PS[:, 6 + t // 2, t % 2 * D:t % 2 * D + D], hT[:, c, t * P:t * P + P],
                                        w["wv"][:, c, :], start=(c == 0), stop=(c == DC - 1))
                ins.then_inc(sm["cc_v"], 1)

                def scores(t):
                    if t:
                        pe.wait_ge(sm["cc_sub2"], t)
                    for g in range(HC):
                        part = slice(32 * g, 32 * g + 32)
                        for ch in range(HC):
                            ins = pe.matmul(PS[:, g, ch * P:ch * P + P], qk[part, 0, ch, t * P:t * P + P],
                                            qk[part, 1, ch, t * P:t * P + P], start=True, stop=True,
                                            tile_position=(32 * g, 0))
                    ins.then_inc(sm["cc_S"], 1)

                pe.wait_ge(sm["cc_qkcp"], 2 * HC)
                scores(0)
                pe.wait_ge(sm["cc_vcp"], 1)
                for t in range(NT):
                    ins = pe.matmul(PS[0:H * NT, 4, 0:D], w["mean_of"][:, t, :], V[:, t, :, 0:AD], start=(t == 0),
                                    stop=(t == NT - 1))
                ins.then_inc(sm["cc_vm"], 1)
                pe.wait_ge(sm["cc_km"], 1)
                for t in range(NT):
                    for ch in range(HC):
                        o = t * H * NT + ch * HC * NT
                        ins = pe.matmul(PS[:, 5, o:o + HC * NT], qk[:, 0, ch, t * P:t * P + P], kb[:, ch, :], start=True,
                                        stop=True)
                ins.then_inc(sm["cc_si"], 1)
                pe.wait_ge(sm["cc_vmcp"], 1)
                pe.wait_ge(sm["cc_ai"], 1)
                for t in range(NT):
                    ins = pe.transpose(PS[0:H * NT, 4, t * P:t * P + P], ai[:, t].rearrange("p h j -> p (h j)"), ident)
                ins.then_inc(sm["cc_aiT"], 1)
                pe.wait_ge(sm["cc_aiTcp"], 1)
                pe.wait_ge(sm["cc_ones"], 1)

                def values(t, g):
                    n = HC * t + g
                    pe.wait_ge(sm["cc_evd" if g % 2 == 0 else "cc_eva"], n // 2 + 1)
                    for ch in range(HC):
                        h = HC * ch + g
                        ins = pe.matmul(PS[:, 6, h * AV:h * AV + AV], pt[:, g % 2, ch * P:ch * P + P], V[:, t, h, :],
                                        start=True, stop=True)
                    ins.then_inc(sm["cc_av"], 1)

                for t in range(NT):
                    if t + 1 < NT:
                        scores(t + 1)
                    if t:
                        pe.wait_ge(sm["cc_Oev"], t)
                    pe.matmul(PS[:, 7, 0:D], aiT[:, t * P:t * P + P], vm[:, :], start=True, stop=True)
                    pe.wait_ge(sm["cc_exp"], t + 1)
                    for g in range(HC):
                        n = HC * t + g
                        if n >= 2:
                            pe.wait_ge(sm["cc_evd" if g % 2 == 0 else "cc_eva"], n // 2)
                        for ch in range(HC):
                            ins = pe.transpose(PS[:, 4 + g % 2, ch * P:ch * P + P], pr[:, t % 2, HC * g + ch, :], ident)
                        ins.then_inc(sm["cc_T"], 1)
                        if g:
                            values(t, g - 1)
                    values(t, HC - 1)
                pe.wait_ge(sm["cc_Oev"], NT)
                for c in range(DC):
                    for t in range(NT):
                        ins = pe.transpose(PS[:, c, t * P:t * P + P], O[:, t, c * P:c * P + P], ident)
                    ins.then_inc(sm["cc_OT"], 1)
                pe.wait_ge(sm["cc_OTcp"], DC)
                for t in range(NT):
                    for c in range(DC):
                        ins = pe.matmul(PS[:, 2 + t // 2, t % 2 * D:t % 2 * D + D], OT[:, c, t * P:t * P + P],
                                        w["wo"][:, c, :], start=(c == 0), stop=(c == DC - 1))
                    if t % 2:
                        ins.then_inc(sm["cc_out"], 1)
        nc.all_engine_barrier(sems_to_clear=sm.all)


KSEL = S // 8
R = KSEL - 1
LM = 1024

CHOICE_SEMS = ("rc_mask rc_pos rc_chain rc_rows rc_Y rc_w rc_wr rc_wb rc_S rc_xs rc_xscp rc_A rc_Acp rc_ms rc_mscp rc_ST "
               "rc_STcp rc_Yst")


def choose_tokens(nc, env, sm, w, b, yT, sel):
    PS, ident, a = env["PS"], env["ident"], env["dram"]
    YW = D + 2
    with ExitStack() as ctx:
        sb = lambda n, s, d=F32: ctx.enter_context(nc.sbuf_tensor("rb_" + n, s, d))
        M, pi = sb("M", [P, NT, S]), sb("pi", [P, NT], I32)
        Y, wr, wb, own = sb("Y", [P, NT, YW]), sb("wr", [1, S]), sb("wb", [P, S]), sb("own", [P, NT, P])
        junk = sb("junk", [P, 3, S])
        gt, eq, ge, rank, wc = (sb(n, [P, NT]) for n in ("gt", "eq", "ge", "rank", "wc"))
        hot, A = sb("hot", [P, NT, R]), sb("A", [P, NT, R])
        with nc.Block() as block:
            @block.sync
            def _(sp):
                sp.dma_start(pi[:, :], a["L1_ffn_position_ids"][bass.ds(b * P, P), :]).then_inc(sm["rc_pos"], 16)
                sp.dma_start(M[:, :, :], a["L1_ffn_attention_mask"][bass.ds(b * LM, S), 0:S]
                             .rearrange("(t p) k -> p t k", p=P)).then_inc(sm["rc_mask"], 16)

            @block.vector
            def _(dve):
                dve.wait_ge(w["loaded"]["rw_in"], 16 * 14)
                link = Chain(dve, sm["rc_chain"])
                dve.wait_ge(sm["rc_rows"], 1)
                for k in range(2):
                    ins = dve.tensor_copy(Y[:, 2 * k:2 * k + 2, 0:D], PS[:, k, :].rearrange("p (t d) -> p t d", d=D))
                ins.then_inc(sm["rc_Y"], 1)
                dve.wait_ge(sm["rc_w"], 1)
                dve.tensor_scalar(wr[:, :], PS[0:1, 2, :], w["router_b"][:, 0:1], None, ALU.add).then_inc(sm["rc_wr"], 1)
                dve.wait_ge(sm["rc_wb"], 1)
                link(dve.tensor_copy(wb[:, :], PS[:, 3, :]))
                link(dve.tensor_tensor(own[:, :, :], wb[:, :].rearrange("p (t k) -> p t k", k=P),
                                       ident.unsqueeze(1).to_broadcast([P, NT, P]), ALU.mult))
                link(dve.tensor_reduce(wc[:, :], own[:, :, :], AX.X, ALU.add))
                for t in range(NT):
                    for n, (op, other, count) in enumerate(((ALU.is_gt, w["ones"][:, :], gt), (ALU.is_ge, w["ones"][:, :], ge),
                                                            (ALU.is_equal, w["before"][:, t, :], eq))):
                        ins = dve.scalar_tensor_tensor(out=junk[:, n, :], in0=wb[:, :], scalar=wc[:, t:t + 1], in1=other,
                                                       op0=op, op1=ALU.mult, accum_out=count[:, t:t + 1])
                    link(ins)
                link(dve.tensor_tensor(rank[:, :], gt[:, :], eq[:, :], ALU.add))
                dve.tensor_scalar(sel["rest"][:, bass.ds(b * NT, NT)], ge[:, :], float(R), None, ALU.is_gt)
                dve.tensor_tensor(hot[:, :, :], w["ranks"][:, :].unsqueeze(1).to_broadcast([P, NT, R]),
                                  rank[:, :].unsqueeze(2).to_broadcast([P, NT, R]), ALU.is_equal)
                dve.tensor_copy(Y[:, :, D + 1], wc[:, :])
                dve.wait_ge(sm["rc_pos"], 16)
                dve.tensor_copy(Y[:, :, D], pi[:, :]).then_inc(sm["rc_S"], 1)
                dve.wait_ge(sm["rc_xs"], 1)
                dve.tensor_copy(sel["xs"][:, bass.ds(b, 1), :], PS[0:R, 4, 0:YW].unsqueeze(1)).then_inc(sm["rc_xscp"], 1)
                dve.wait_ge(sm["rc_A"], 1)
                dve.tensor_copy(A[:, :, :], PS[:, 5, 0:NT * R].rearrange("p (t r) -> p t r", t=NT)).then_inc(sm["rc_Acp"], 1)
                dve.wait_ge(sm["rc_ms"], 1)
                dve.tensor_copy(sel["ms"][:, bass.ds(b, 1), :], PS[0:R, 6, 0:R].unsqueeze(1)).then_inc(sm["rc_mscp"], 1)
                dve.wait_ge(sm["rc_ST"], 1)
                dve.tensor_copy(sel["ST"][:, bass.ds(b, 1), :], PS[0:R, 7, :].unsqueeze(1)).then_inc(sm["rc_STcp"], 1)

            @block.scalar
            def _(act):
                act.wait_ge(sm["rc_Y"], 1)
                act.activation(sel["Y"][:, bass.ds(b * NT, NT), :], Y[:, :, 0:D], ACT.Copy).then_inc(sm["rc_Yst"], 1)

            @block.tensor
            def _(pe):
                pe.wait_ge(w["loaded"]["rw_in"], 16 * 14)
                for t in range(NT):
                    for c in range(DC):
                        ins = pe.transpose(PS[:, t // 2, t % 2 * D + c * P:t % 2 * D + c * P + P], yT[:, c, t * P:t * P + P],
                                           ident)
                ins.then_inc(sm["rc_rows"], 1)
                for c in range(DC):
                    ins = pe.matmul(PS[0:1, 2, :], w["router"][:, c:c + 1], yT[:, c, :], start=(c == 0), stop=(c == DC - 1))
                ins.then_inc(sm["rc_w"], 1)
                pe.wait_ge(sm["rc_wr"], 1)
                pe.matmul(PS[:, 3, :], w["ones"][0:1, 0:P], wr[:, :], start=True, stop=True).then_inc(sm["rc_wb"], 1)
                pe.wait_ge(sm["rc_S"], 1)
                for t in range(NT):
                    ins = pe.matmul(PS[0:R, 4, 0:YW], hot[:, t, :], Y[:, t, :], start=(t == 0), stop=(t == NT - 1))
                ins.then_inc(sm["rc_xs"], 1)
                pe.wait_ge(sm["rc_mask"], 16)
                for kt in range(NT):
                    for t in range(NT):
                        ins = pe.matmul(PS[:, 5, kt * R:kt * R + R], M[:, t, kt * P:kt * P + P], hot[:, t, :],
                                        start=(t == 0), stop=(t == NT - 1))
                ins.then_inc(sm["rc_A"], 1)
                for t in range(NT):
                    ins = pe.transpose(PS[0:R, 7, t * P:t * P + P], hot[:, t, :], ident)
                ins.then_inc(sm["rc_ST"], 1)
                pe.wait_ge(sm["rc_Acp"], 1)
                for kt in range(NT):
                    ins = pe.matmul(PS[0:R, 6, 0:R], A[:, kt, :], hot[:, kt, :], start=(kt == 0), stop=(kt == NT - 1))
                ins.then_inc(sm["rc_ms"], 1)
        nc.all_engine_barrier(sems_to_clear=sm.all)


def routed_weights(nc, env, ctx):
    sb = lambda n, s, d=F32: ctx.enter_context(nc.sbuf_tensor("rw_" + n, s, d))
    w = {n: sb(n, [P, DC, D]) for n in ("wq", "wk", "wv", "wo")}
    w.update(w1=sb("w1", [P, DC, DF]), w2=sb("w2", [P, FC, D]), ln1=sb("ln1", [P, DC]), ln2=sb("ln2", [P, DC]),
             router=sb("router", [P, DC]), router_b=sb("router_b", [1, 1]), ones=sb("ones", [P, S]),
             before=sb("before", [P, NT, S]), ranks=sb("ranks", [P, R]), inv=sb("inv", [P, AD // 2]))
    w["loaded"] = env["loads"]
    return w


def routed_loads(nc, env, w):
    a, sm = env["dram"], w["loaded"]
    with nc.Block() as block:
        @block.sync
        def _(sp):
            def load(dst, src):
                sp.dma_start(dst, src).then_inc(sm["rw_in"], 16)

            for n in ("wq", "wk", "wv", "wo", "w1", "w2"):
                load(w[n][:, :, :], a["L1_ffn_" + n].rearrange("(c p) n -> p c n", p=P))
            load(w["ln1"][:, :], a["L1_ffn_ln1"])
            load(w["ln2"][:, :], a["L1_ffn_ln2"])
            load(w["router"][:, :], a["L1_ffn_router_w"])
            load(w["router_b"][:, :], a["L1_ffn_router_b"].unsqueeze(0))
            load(w["ones"][:, :], a["c_ones"])
            load(w["before"][:, :, :], a["c_before"])
            load(w["ranks"][:, :], a["c_ranks"])
            load(w["inv"][:, :], a["c_inv"])


TWO_PI = 2 * np.pi
TP_HIGH = 6.28125
TP_LOW = float(TWO_PI - TP_HIGH)
PI_F = float(np.float32(3.1415925))
MAGIC = float(1.5 * 2 ** 23)


def routed_block(nc, env, w, sel, out):
    X, PS, ident = env["X"], env["PS"], env["ident"]
    AV, HD = AD + 1, AD // 2
    RB = B * R
    xs, ms, ST, Y, rest = sel["xs"], sel["ms"], sel["ST"], sel["Y"], sel["rest"]
    with ExitStack() as ctx:
        sb = lambda n, s, d=F32: ctx.enter_context(nc.sbuf_tensor("rr_" + n, s, d))
        sm = Sems(ctx, nc, "rr_chain rr_ss rr_std rr_hn rr_T rr_hnT rr_qkv rr_ang rr_sin rr_rope rr_qkT rr_qkTcp rr_S rr_sub "
                           "rr_exp rr_pT rr_pTcp rr_av rr_o rr_oT rr_oTcp rr_wo rr_h1 rr_g rr_h2 rr_proc rr_sc rr_row "
                           "rr_store")
        sq, hn, hnT = sb("sq", [R, D]), sb("hn", [R, B, D]), sb("hnT", [P, DC, RB])
        ss, rr = sb("ss", [R, B]), sb("rr", [R, B])
        f, n, r, rc = (sb(k, [R, B, HD]) for k in ("f", "n", "r", "rc"))
        sin, cos = sb("sin", [R, B, HD]), sb("cos", [R, B, HD])
        ta, tb = sb("ta", [R, 2, B * H * HD]), sb("tb", [R, 2, B * H * HD])
        qp, V = sb("qp", [R, 2, B, H, 32]), sb("V", [R, B, H, AV])
        qkT = sb("qkT", [P, 2, B, HC, R])
        sc, mx, pr, pT = sb("sc", [R, 2, H, R]), sb("mx", [R, H]), sb("pr", [R, 2, H, R]), sb("pT", [R, 2, H, R])
        rden, o, x1 = sb("rden", [R, H]), sb("o", [R, B, D]), sb("x1", [R, B, D])
        g = sb("g", [P, FC, RB])
        xo = sb("xo", [P, B * NT, D])
        rows = lambda bank: PS[0:R, bank:bank + 2, :].rearrange("p a (t d) -> p (a t) d", d=D)
        halves = lambda k: rows(2 * k).rearrange("p b (h e d) -> p (b h) e d", e=2, d=HD)

        with nc.Block() as block:
            @block.vector
            def _(dve):
                link = Chain(dve, sm["rr_chain"])

                def rms(src, k):
                    for b in range(B):
                        link(dve.tensor_tensor_reduce(out=sq[:, :], in0=src(b), in1=src(b), scale=1.0, scalar=0.0,
                                                      op0=ALU.mult, op1=ALU.add, accum_out=ss[:, b:b + 1]))
                    dve.tensor_scalar(ss[:, :], ss[:, :], 1 / D, 1e-6, ALU.mult, ALU.add).then_inc(sm["rr_ss"], 1)
                    dve.wait_ge(sm["rr_std"], k + 1)
                    link(dve.reciprocal(rr[:, :], ss[:, :]))
                    for b in range(B):
                        ins = dve.tensor_scalar(hn[:, b, :], src(b), rr[:, b:b + 1], None, ALU.mult)
                    ins.then_inc(sm["rr_hn"], 1)
                    for c in range(DC):
                        dve.wait_ge(sm["rr_T"], DC * k + c + 1)
                        dve.tensor_scalar(hnT[:, c, :], PS[:, 6 + c, 0:RB], w["ln2" if k else "ln1"][:, c:c + 1], None,
                                          ALU.mult).then_inc(sm["rr_hnT"], 1)

                link(dve.tensor_tensor(f[:, :, :], xs[:, :, D:D + 1].to_broadcast([R, B, HD]),
                                       w["inv"][0:R, :].unsqueeze(1).to_broadcast([R, B, HD]), ALU.mult))
                link(dve.tensor_scalar(n[:, :, :], f[:, :, :], 1 / TWO_PI, MAGIC, ALU.mult, ALU.add))
                link(dve.tensor_scalar(n[:, :, :], n[:, :, :], MAGIC, None, ALU.subtract))
                link(dve.scalar_tensor_tensor(out=r[:, :, :], in0=n[:, :, :], scalar=-TP_HIGH, in1=f[:, :, :], op0=ALU.mult,
                                              op1=ALU.add))
                link(dve.scalar_tensor_tensor(out=r[:, :, :], in0=n[:, :, :], scalar=-TP_LOW, in1=r[:, :, :], op0=ALU.mult,
                                              op1=ALU.add))
                link(dve.tensor_scalar(rc[:, :, :], r[:, :, :], float(np.pi / 2), None, ALU.add))
                link(dve.tensor_scalar(n[:, :, :], rc[:, :, :], PI_F, -TWO_PI, ALU.is_gt, ALU.mult))
                link(dve.tensor_tensor(rc[:, :, :], rc[:, :, :], n[:, :, :], ALU.add))
                link(dve.tensor_scalar(r[:, :, :], r[:, :, :], PI_F, -PI_F, ALU.min, ALU.max))
                dve.tensor_scalar(rc[:, :, :], rc[:, :, :], PI_F, -PI_F, ALU.min, ALU.max).then_inc(sm["rr_ang"], 1)
                link(dve.memset(qp[:, :, :, :, :], 0.0))
                link(dve.memset(V[:, :, :, AD], 1.0))
                rms(lambda b: xs[:, b, 0:D], 0)
                dve.wait_ge(sm["rr_qkv"], 3)
                dve.wait_ge(sm["rr_sin"], 1)
                for b in range(B):
                    ins = dve.tensor_copy(V[:, b, :, 0:AD], rows(4)[:, b, :].rearrange("p (h d) -> p h d", d=AD))
                link(ins)
                spread = lambda v: v[:, :, :].unsqueeze(2).to_broadcast([R, B, H, HD])
                wide = lambda v, i: v[:, i, :].rearrange("p (b h d) -> p b h d", b=B, d=HD)
                for k in range(2):
                    lo = rows(2 * k).rearrange("p b (h e d) -> p b h e d", e=2, d=HD)[:, :, :, 0, :]
                    hi = rows(2 * k).rearrange("p b (h e d) -> p b h e d", e=2, d=HD)[:, :, :, 1, :]
                    for i, (x, y) in enumerate(((lo, hi), (hi, lo))):
                        dve.tensor_tensor(wide(ta, i), x, spread(cos), ALU.mult)
                        link(dve.tensor_tensor(wide(tb, i), y, spread(sin), ALU.mult))
                        link(dve.tensor_tensor(wide(ta, i), wide(ta, i), wide(tb, i), (ALU.subtract, ALU.add)[i]))
                        ins = dve.tensor_scalar(qp[:, k, :, :, HD * i:HD * i + HD].rearrange("p b h d -> p (b h) d"),
                                                ta[:, i, :].rearrange("p (h d) -> p h d", d=HD),
                                                0.25 if k == 0 else 1.0, None, ALU.mult)
                    ins.then_inc(sm["rr_rope"], 1)
                for k in range(2):
                    for b2 in range(2):
                        dve.wait_ge(sm["rr_qkT"], 2 * k + b2 + 1)
                        bank = 6 + b2
                        for e in range(2):
                            ins = dve.tensor_copy(qkT[:, k, 2 * b2 + e],
                                                  PS[:, bank, e * 256:e * 256 + HC * R].rearrange("p (c r) -> p c r", c=HC))
                        ins.then_inc(sm["rr_qkTcp"], 1)
                for b in range(B):
                    dve.wait_ge(sm["rr_S"], b + 1)
                    s4 = PS[0:R, 0:4, 0:HC * R].rearrange("p g (c r) -> p g c r", r=R)
                    v4 = sc[:, b % 2].rearrange("p (g c) r -> p g c r", c=HC)
                    if b >= 2:
                        dve.wait_ge(sm["rr_exp"], b - 1)
                    for gg in range(HC):
                        ins = dve.tensor_tensor(v4[:, gg], s4[:, gg], ms[:, b, :].unsqueeze(1).to_broadcast([R, HC, R]),
                                                ALU.add)
                    link(ins)
                    link(dve.tensor_reduce(mx[:, :], sc[:, b % 2], AX.X, ALU.max))
                    dve.tensor_tensor(sc[:, b % 2], sc[:, b % 2], mx[:, :].unsqueeze(2).to_broadcast([R, H, R]),
                                      ALU.subtract).then_inc(sm["rr_sub"], 1)
                    dve.wait_ge(sm["rr_pT"], b + 1)
                    for k in range(2):
                        ins = dve.tensor_copy(pT[:, b % 2, 8 * k:8 * k + 8, :],
                                              PS[0:R, 4 + k, 0:8 * R].rearrange("p (h r) -> p h r", r=R))
                    ins.then_inc(sm["rr_pTcp"], 1)
                    dve.wait_ge(sm["rr_av"], b + 1)
                    inside = PS[0:R, 6 + b % 2, 0:H * AV].rearrange("p (h d) -> p h d", d=AV)
                    link(dve.reciprocal(rden[:, :], inside[:, :, AD]))
                    dve.tensor_tensor(o[:, b, :].rearrange("p (h d) -> p h d", d=AD), inside[:, :, 0:AD],
                                      rden[:, :].unsqueeze(2).to_broadcast([R, H, AD]), ALU.mult).then_inc(sm["rr_o"], 1)
                for c in range(DC):
                    dve.wait_ge(sm["rr_oT"], c + 1)
                    dve.tensor_copy(hnT[:, c, :], PS[:, c, 0:RB]).then_inc(sm["rr_oTcp"], 1)
                dve.wait_ge(sm["rr_wo"], 1)
                link(dve.tensor_tensor(x1[:, :, :], rows(2), xs[:, :, 0:D], ALU.add))
                rms(lambda b: x1[:, b, :], 1)
                dve.wait_ge(sm["rr_h2"], 1)
                link(dve.tensor_tensor(x1[:, :, :], rows(2), x1[:, :, :], ALU.add))
                for b in range(B):
                    ins = dve.tensor_scalar(o[:, b, :], x1[:, b, :], xs[:, b, D + 1:D + 2], None, ALU.mult)
                ins.then_inc(sm["rr_proc"], 1)
                for t in range(B * NT):
                    dve.wait_ge(sm["rr_sc"], t + 1)
                    link(dve.scalar_tensor_tensor(out=xo[:, t, :], in0=Y[:, t, :], scalar=rest[:, t:t + 1],
                                                  in1=PS[:, t % 4, 0:D], op0=ALU.mult, op1=ALU.add))
                    dve.tensor_tensor(xo[:, t, :], xo[:, t, :], X[:, t, :], ALU.add).then_inc(sm["rr_row"], 1)

            @block.scalar
            def _(act):
                act.wait_ge(sm["rr_ang"], 1)
                act.activation(sin[:, :, :], r[:, :, :], ACT.Sin)
                act.activation(cos[:, :, :], rc[:, :, :], ACT.Sin).then_inc(sm["rr_sin"], 1)
                act.wait_ge(sm["rr_ss"], 1)
                act.activation(ss[:, :], ss[:, :], ACT.Sqrt).then_inc(sm["rr_std"], 1)
                for b in range(B):
                    act.wait_ge(sm["rr_sub"], b + 1)
                    if b >= 2:
                        act.wait_ge(sm["rr_pT"], b - 1)
                    act.activation(pr[:, b % 2], sc[:, b % 2], ACT.Exp).then_inc(sm["rr_exp"], 1)
                act.wait_ge(sm["rr_ss"], 2)
                act.activation(ss[:, :], ss[:, :], ACT.Sqrt).then_inc(sm["rr_std"], 1)
                for m in range(FC):
                    act.wait_ge(sm["rr_h1"], m + 1)
                    act.activation(g[:, m, :], PS[:, m % 2, 0:RB], ACT.Gelu_apprx_tanh).then_inc(sm["rr_g"], 1)

            @block.sync
            def _(sp):
                o4 = out.rearrange("b (t p) d -> b p t d", p=P)
                for b in range(B):
                    sp.wait_ge(sm["rr_row"], NT * (b + 1))
                    sp.dma_start(o4[b], xo[:, NT * b:NT * b + NT, :]).then_inc(sm["rr_store"], 16)
                sp.wait_ge(sm["rr_store"], 16 * B)

            @block.tensor
            def _(pe):
                idr = ident[0:R, 0:R]

                def turned(src, bank, done):
                    for c in range(DC):
                        for b in range(B):
                            ins = pe.transpose(PS[:, bank + c, b * R:b * R + R], src[:, b, c * P:c * P + P], idr)
                        ins.then_inc(sm[done], 1)

                pe.wait_ge(sm["rr_hn"], 1)
                turned(hn, 6, "rr_T")
                pe.wait_ge(sm["rr_hnT"], DC)
                for k, name in enumerate(("wq", "wk", "wv")):
                    for b in range(B):
                        for c in range(DC):
                            ins = pe.matmul(PS[0:R, 2 * k + b // 2, b % 2 * D:b % 2 * D + D], hnT[:, c, b * R:b * R + R],
                                            w[name][:, c, :], start=(c == 0), stop=(c == DC - 1))
                    ins.then_inc(sm["rr_qkv"], 1)
                for k in range(2):
                    pe.wait_ge(sm["rr_rope"], k + 1)
                    for b2 in range(2):
                        if k:
                            pe.wait_ge(sm["rr_qkTcp"], b2 + 1)
                        for e in range(2):
                            for ch in range(HC):
                                o0 = e * 256 + ch * R
                                ins = pe.transpose(PS[:, 6 + b2, o0:o0 + R],
                                                   qp[:, k, 2 * b2 + e, HC * ch:HC * ch + HC, :].rearrange("p h d -> p (h d)"),
                                                   idr)
                        ins.then_inc(sm["rr_qkT"], 1)
                pe.wait_ge(sm["rr_qkTcp"], 4)
                for b in range(B):
                    if b:
                        pe.wait_ge(sm["rr_sub"], b)
                    for gg in range(HC):
                        part = slice(32 * gg, 32 * gg + 32)
                        for ch in range(HC):
                            ins = pe.matmul(PS[0:R, gg, ch * R:ch * R + R], qkT[part, 0, b, ch, :], qkT[part, 1, b, ch, :],
                                            start=True, stop=True, tile_position=(32 * gg, 0))
                    ins.then_inc(sm["rr_S"], 1)
                    pe.wait_ge(sm["rr_exp"], b + 1)
                    if b:
                        pe.wait_ge(sm["rr_pTcp"], b)
                    for i in range(H):
                        ins = pe.transpose(PS[0:R, 4 + i // 8, i % 8 * R:i % 8 * R + R], pr[:, b % 2, i, :], idr)
                    ins.then_inc(sm["rr_pT"], 1)
                    pe.wait_ge(sm["rr_pTcp"], b + 1)
                    if b >= 2:
                        pe.wait_ge(sm["rr_o"], b - 1)
                    for i in range(H):
                        h = HC * (i % HC) + i // HC
                        ins = pe.matmul(PS[0:R, 6 + b % 2, h * AV:h * AV + AV], pT[:, b % 2, i, :], V[:, b, h, :],
                                        start=True, stop=True)
                    ins.then_inc(sm["rr_av"], 1)
                pe.wait_ge(sm["rr_o"], B)
                turned(o, 0, "rr_oT")
                pe.wait_ge(sm["rr_oTcp"], DC)
                for b in range(B):
                    for c in range(DC):
                        ins = pe.matmul(PS[0:R, 2 + b // 2, b % 2 * D:b % 2 * D + D], hnT[:, c, b * R:b * R + R],
                                        w["wo"][:, c, :], start=(c == 0), stop=(c == DC - 1))
                ins.then_inc(sm["rr_wo"], 1)
                pe.wait_ge(sm["rr_hn"], 2)
                turned(hn, 6, "rr_T")
                pe.wait_ge(sm["rr_hnT"], 2 * DC)
                for m in range(FC):
                    if m >= 2:
                        pe.wait_ge(sm["rr_g"], m - 1)
                    for c in range(DC):
                        ins = pe.matmul(PS[:, m % 2, 0:RB], w["w1"][:, c, m * P:m * P + P], hnT[:, c, :], start=(c == 0),
                                        stop=(c == DC - 1))
                    ins.then_inc(sm["rr_h1"], 1)
                pe.wait_ge(sm["rr_g"], FC)
                for b in range(B):
                    for k in range(FC):
                        ins = pe.matmul(PS[0:R, 2 + b // 2, b % 2 * D:b % 2 * D + D], g[:, k, b * R:b * R + R],
                                        w["w2"][:, k, :], start=(k == 0), stop=(k == FC - 1))
                ins.then_inc(sm["rr_h2"], 1)
                pe.wait_ge(sm["rr_proc"], 1)
                for t in range(B * NT):
                    if t >= 4:
                        pe.wait_ge(sm["rr_row"], t - 3)
                    b = t // NT
                    pe.matmul(PS[:, t % 4, 0:D], ST[:, b, t % NT * P:t % NT * P + P], o[:, b, :], start=True,
                              stop=True).then_inc(sm["rr_sc"], 1)
        nc.all_engine_barrier(sems_to_clear=sm.all)


def program(nc, a, out):
    with ExitStack() as ctx:
        sb = lambda n, s, d=F32: ctx.enter_context(nc.sbuf_tensor(n, s, d))
        env = {"dram": a, "loads": Sems(ctx, nc, "fw_in rw_in")}
        env["PS"] = ctx.enter_context(nc.psum_tensor("PS", [P, 8, 512], F32))
        X = env["X"] = sb("X", [P, B * NT, D])
        env["hT"] = sb("hT", [P, DC, S])
        env["rel"] = nc.dram_tensor("rel_table", [H, P, S], F32).ap()
        cI, cHalf = sb("ident", [P, P]), sb("half_ones", [P, P])
        cHo, cOr = sb("head_of", [P, MC, H]), sb("of_head", [H, MC, P], F32R)
        cCm, cCmb, cIb = sb("causal", [P, P]), sb("causal_bf", [P, P], BF16), sb("ident_bf", [P, P], BF16)
        env.update(ident=cI[:, :], half_ones=cHalf[:, :], head_of=cHo, of_head=cOr, causal_bf=cCmb[:, :],
                   ident_bf=cIb[:, :])
        with ExitStack() as inner:
            sm = Sems(inner, nc, "in_loads in_cast")
            cOh = inner.enter_context(nc.sbuf_tensor("of_head_f32", [H, MC, P], F32))
            with nc.Block() as block:
                @block.sync
                def _(sp):
                    for dst, src in ((cI[:, :], a["c_ident"]), (cHalf[:, :], a["c_half_ones"]),
                                     (cHo[:, :, :], a["c_head_of"]), (cOh[:, :, :], a["c_of_head"]),
                                     (cCm[:, :], a["c_causal"]),
                                     (X[:, :, :], a["x"].rearrange("b (t p) d -> p (b t) d", p=P))):
                        sp.dma_start(dst, src).then_inc(sm["in_loads"], 16)

                @block.vector
                def _(dve):
                    dve.wait_ge(sm["in_loads"], 6 * 16)
                    dve.tensor_copy(cOr[:, :, :], cOh[:, :, :]).then_inc(sm["in_cast"], 1)
                    dve.tensor_copy(cIb[:, :], cI[:, :]).then_inc(sm["in_cast"], 1)
                    dve.tensor_copy(cCmb[:, :], cCm[:, :]).then_inc(sm["in_cast"], 1)
                    dve.wait_ge(sm["in_cast"], 3)
            nc.all_engine_barrier(sems_to_clear=sm.all)
        relative_positions(nc, env)
        with ExitStack() as hctx:
            env["hTs"] = hctx.enter_context(nc.sbuf_tensor("hTs", [P, B * DC, S], F32))
            with ExitStack() as lctx:
                w = cond_attention_weights(nc, env, lctx, 0)
                sm = Sems(lctx, nc, COND_SEMS)
                with nc.Fori(0, B) as b:
                    cond_attention(nc, env, sm, w, b, 0)
            with ExitStack() as lctx:
                wg = gated_attention_weights(nc, env, lctx)
                smg = Sems(lctx, nc, GATED_SEMS)
                with nc.Fori(0, B) as b:
                    gated_attention(nc, env, smg, wg, b)
        with ExitStack() as lctx:
            w, wf = experts_weights(nc, env, lctx, 0), ffn_weights(nc, env, lctx)
            sm, smf = Sems(lctx, nc, EXPERT_SEMS), Sems(lctx, nc, FFN_SEMS)
            with nc.Fori(0, B) as b:
                experts(nc, env, sm, w, b, env["hT"], 0)
                ffn(nc, env, smf, wf, b, env["hT"])
        with ExitStack() as lctx:
            w = cond_attention_weights(nc, env, lctx, 1)
            wc = chunked_attention_weights(nc, env, lctx)
            sm, smc = Sems(lctx, nc, COND_SEMS), Sems(lctx, nc, CHUNKED_SEMS)
            with nc.Fori(0, B) as b:
                cond_attention(nc, env, sm, w, b, 1)
                chunked_attention(nc, env, smc, wc, b)
        with ExitStack() as lctx:
            sb = lambda n, s, d=F32: lctx.enter_context(nc.sbuf_tensor(n, s, d))
            sel = {"xs": sb("sel_xs", [R, B, D + 2]), "ms": sb("sel_ms", [R, B, R]), "ST": sb("sel_ST", [R, B, S]),
                   "Y": sb("sel_Y", [P, B * NT, D]), "rest": sb("sel_rest", [P, B * NT])}
            wr = routed_weights(nc, env, lctx)
            with ExitStack() as inner:
                w = experts_weights(nc, env, inner, 1)
                routed_loads(nc, env, wr)
                sm, smr = Sems(inner, nc, EXPERT_SEMS), Sems(inner, nc, CHOICE_SEMS)
                with nc.Fori(0, B) as b:
                    experts(nc, env, sm, w, b, env["hT"], 1)
                    choose_tokens(nc, env, smr, wr, b, env["hT"], sel)
            routed_block(nc, env, wr, sel, out)
        nc.all_engine_barrier(sems_to_clear=env["loads"].all)


def shape_constants():
    c = {}
    p = np.arange(P)
    c["c_ident"] = np.eye(P, dtype=np.float32)
    c["c_half_ones"] = (p[:, None] // DH == p[None, :] // DH).astype(np.float32)
    head = (np.arange(MC)[:, None] * 2 + p[None, :] // DH)
    c["c_head_of"] = (head.T[:, :, None] == np.arange(H)).astype(np.float32)
    c["c_of_head"] = np.ascontiguousarray(c["c_head_of"].transpose(2, 1, 0))
    c["c_causal"] = np.where(p[None, :] > p[:, None], np.float32(NEG), np.float32(0)).astype(np.float32)
    c["c_pos"] = (511 - (np.arange(NPOS // P)[None, :] * P + p[:, None])).astype(np.float32)
    g, r, k = p // 32, p % 32, np.arange(S)
    c["c_blocks"] = (k[None, :] // 64 == np.arange(NB)[:, None]).astype(np.float32)
    c["c_key_rows"] = (r[None, :] == AD + np.arange(NB)[:, None]).astype(np.float32)
    c["c_head4"] = ((g[:, None, None] + HC * np.arange(HC)[None, :, None] == np.arange(H)) & (r < AD)[:, None, None]).astype(np.float32)
    pg = np.arange(GR)
    ph, pn = pg // NB % GH, pg % NB
    hk, kk = np.arange(GH * NT) // NT, np.arange(GH * NT) % NT
    c["c_pick"] = ((ph[:, None, None] == hk[None, :, None])
                   & (pn[:, None, None] == 2 * kk[None, :, None] + p[None, None, :] // 64)).astype(np.float32)
    c["c_tile_of"] = (pg[:, None] // (GH * NB) == np.arange(NT)).astype(np.float32)
    block = p // 32
    c["c_spread"] = np.zeros((P, 4, HC, P), np.float32)
    for which, blocks in enumerate(((0, 1), (2, 3), (0, 2), (1, 3))):
        for of in range(HC):
            c["c_spread"][:, which, of] = ((r[:, None] == r[None, :]) & (block[:, None] == of)
                                           & np.isin(block, blocks)[None, :])
    c["c_own_block"] = (2 * np.arange(NT)[None, :, None] + p[:, None, None] // 64 == np.arange(NB)).astype(np.float32)
    c["c_first"] = np.tile((NE - np.arange(NE)).astype(np.float32), (P, 1))
    c["c_row_of"] = np.repeat(np.eye(NE, dtype=np.float32)[:, :, None], P, axis=2)
    hj = np.arange(H * NT)
    c["c_mean_of"] = np.broadcast_to((hj[None, :] % NT == np.arange(NT)[:, None]) / np.float32(P),
                                     (P, NT, H * NT)).astype(np.float32)
    c["c_head_rows"] = (hj[:, None] // NT == np.arange(D)[None, :] // AD).astype(np.float32)
    later = np.arange(NT)[None, :] > np.arange(NT)[:, None]
    c["c_later"] = np.broadcast_to(np.where(later, NEG, 0.0), (P, NT, NT)).astype(np.float32)
    c["c_ones"] = np.ones((P, S), np.float32)
    i = np.arange(NT)[None, :] * P + p[:, None]
    c["c_before"] = (k[None, None, :] < i[:, :, None]).astype(np.float32)
    c["c_ranks"] = np.tile(np.arange(R, dtype=np.float32), (P, 1))
    exponent = np.arange(0, AD, 2, dtype=np.float32) / np.float32(AD)
    c["c_inv"] = np.tile(np.float32(1.0) / np.float32(10000.0) ** exponent, (P, 1)).astype(np.float32)
    c["c_eye8"] = np.eye(NB, dtype=np.float32)
    return c


TRANSPOSED = ("L0_attn_wq", "L0_attn_wk", "L0_attn_wv", "L0_attn_wo", "L0_cond2_wt", "L0_cond2_wg",
              "L0_ffn_w1_w", "L0_ffn_w2_w", "L0_ffn_h1_w", "L0_ffn_h2_w", "L0_ffn_w3_w",
              "L1_attn_wq", "L1_attn_wk", "L1_attn_wv", "L1_attn_wo", "L1_cond2_wt", "L1_cond2_wg")


COLUMNS = ("L0_cond_g_norm", "L0_cond_g_out", "L1_cond_g_in", "L1_cond_g_out", "L0_ffn_w1_s", "L0_ffn_w2_s",
           "L0_ffn_h1_s", "L0_ffn_h2_s", "L1_ffn_router_w", "L1_ffn_ln1", "L1_ffn_ln2")


def kernel(**inputs):
    import concourse.bacc as bacc
    from concourse.bass_utils import run_bass_kernel_spmd

    nc = bacc.Bacc("TRN2", target_bir_lowering=False, num_devices=1)
    arrays, aps = {}, {}
    host = {k: np.asarray(v) for k, v in inputs.items()}
    for name in TRANSPOSED:
        host[name] = host[name].T
    for name in COLUMNS:
        host[name] = host[name].reshape(-1, P).T
    for name in ("L1_attn_bq", "L1_attn_bk"):
        host[name] = host[name].reshape(HC, HC, AD).transpose(1, 2, 0)
    host["L1_ffn_attention_mask"] = host["L1_ffn_attention_mask"].reshape(B * LM, LM)
    host["L1_ffn_position_ids"] = host["L1_ffn_position_ids"][:, :S].reshape(B, NT, P).transpose(0, 2, 1).reshape(B * P, NT)
    host["cond_columns"] = host["cond_64"].T
    host.update(shape_constants())
    for name, v in host.items():
        v = np.ascontiguousarray(v)
        arrays["in_" + name] = v
        aps[name] = nc.dram_tensor("in_" + name, v.shape, mybir.dt.from_np(v.dtype), kind="ExternalInput").ap()
    out = nc.dram_tensor("out", (B, S, D), F32, kind="ExternalOutput").ap()
    program(nc, aps, out)
    result = run_bass_kernel_spmd(nc, [arrays], core_ids=[0])
    return result.results[0]["out"]
```
